# Optimizing a Trainium2 kernel written in Bass

```python
import numpy as np
import jax
import jax.numpy as jnp

def _softmax(x, axis=-1):
    return jax.nn.softmax(x, axis=axis)

def _gelu(x):
    return jax.nn.gelu(x, approximate=True)

def _silu(x):
    return jax.nn.silu(x)

def _sigmoid(x):
    return jax.nn.sigmoid(x)

def _layernorm(x, axis=-1, eps=1e-05):
    m = jnp.mean(x, axis=axis, keepdims=True)
    v = jnp.var(x, axis=axis, keepdims=True)
    return (x - m) / jnp.sqrt(v + eps)

def _scatter_add(tgt, idx, src, axis=0):
    return tgt.at[idx].add(src)

def _segment_sum(src, seg, n):
    return jax.ops.segment_sum(src, seg, n)
kernel_name = 'mk_gnn_ffn_d1_gnn_r32_644bda'

def setup_inputs(seed: int=0):
    np.random.seed(seed)
    _w = jnp.asarray

    def _rec_inputs():
        import jax
        import jax.numpy as jnp
        _gk = jax.random.key(seed)
        x = -0.0002117 + 1 * jax.random.normal(jax.random.fold_in(_gk, 1), (3125, 256), jnp.float32)
        _s = jax.random.randint(jax.random.fold_in(_gk, 2), (25000,), 0, 3125, jnp.int32)
        _d = jax.random.randint(jax.random.fold_in(_gk, 3), (25000,), 0, 3125, jnp.int32)
        _loop = jnp.arange(3125, dtype=jnp.int32)
        src = jnp.concatenate([_s, _d, _loop])
        dst = jnp.concatenate([_d, _s, _loop])
        _o = jnp.argsort(dst, stable=True)
        src = src[_o]
        dst = dst[_o]
        edge_weight = jax.random.uniform(jax.random.fold_in(_gk, 12), (53125,), jnp.float32, 0.0, 1)
        return (x, src, dst, edge_weight)
    x, src, dst, edge_weight = _rec_inputs()

    def _L0_gnn_setup():
        import jax, jax.numpy as jnp
        import numpy as np
        N = 3125
        E = 100000
        D_IN = 256
        D_OUT = 256
        key = jax.random.key(seed)
        k = jax.random.split(key, 8)
        stdv = 1.0 / np.sqrt(D_OUT)
        x = jax.random.normal(k[0], (N, D_IN), dtype=jnp.float32)
        edge_row = jax.random.randint(k[1], (E,), 0, N, dtype=jnp.int32)
        edge_col = jax.random.randint(k[2], (E,), 0, N, dtype=jnp.int32)
        edge_val = jax.random.uniform(k[3], (E,), dtype=jnp.float32)
        weight_l = jax.random.uniform(k[4], (D_IN, D_OUT), minval=-stdv, maxval=stdv, dtype=jnp.float32)
        bias_l = jax.random.uniform(k[5], (D_OUT,), minval=-stdv, maxval=stdv, dtype=jnp.float32)
        weight_r = jax.random.uniform(k[6], (D_IN, D_OUT), minval=-stdv, maxval=stdv, dtype=jnp.float32)
        bias_r = jax.random.uniform(k[7], (D_OUT,), minval=-stdv, maxval=stdv, dtype=jnp.float32)
        return {'x': x, 'edge_row': edge_row, 'edge_col': edge_col, 'edge_val': edge_val, 'weight_l': weight_l, 'bias_l': bias_l, 'weight_r': weight_r, 'bias_r': bias_r}
    _L0_gnn_all = _L0_gnn_setup()
    _L0_gnn_in = {k: v for k, v in _L0_gnn_all.items() if k in ('weight_l', 'bias_l', 'weight_r', 'bias_r')}
    del _L0_gnn_all

    def _L0_ffn_setup():
        import math
        import jax, jax.numpy as jnp
        import numpy as np
        CAPACITY_FACTOR = 1.25
        key = jax.random.key(seed)
        ks = jax.random.split(key, 5)
        B, L, D, F, E = (8, 256, 256, 1024, 8)
        h = jax.random.normal(ks[0], (B, L, D), dtype=jnp.float32)
        gate_w = jax.random.normal(ks[1], (D, E), dtype=jnp.float32) * 0.02
        gate_b = jnp.zeros((E,), dtype=jnp.float32)
        w1 = jax.random.normal(ks[2], (E, D, F), dtype=jnp.float32) * (1.0 / math.sqrt(D))
        b1 = jnp.zeros((E, F), dtype=jnp.float32)
        w2 = jax.random.normal(ks[3], (E, F, D), dtype=jnp.float32) * (1.0 / math.sqrt(F))
        b2 = jnp.zeros((E, D), dtype=jnp.float32)
        return {'h': h, 'gate_w': gate_w, 'gate_b': gate_b, 'w1': w1, 'b1': b1, 'w2': w2, 'b2': b2}
    _L0_ffn_all = _L0_ffn_setup()
    _L0_ffn_in = {k: v for k, v in _L0_ffn_all.items() if k in ('gate_w', 'gate_b', 'w1', 'b1', 'w2', 'b2')}
    del _L0_ffn_all
    return {'x': x, 'src': src, 'dst': dst, 'edge_weight': edge_weight, 'L0_gnn_weight_l': _L0_gnn_in['weight_l'], 'L0_gnn_bias_l': _L0_gnn_in['bias_l'], 'L0_gnn_weight_r': _L0_gnn_in['weight_r'], 'L0_gnn_bias_r': _L0_gnn_in['bias_r'], 'L0_ffn_gate_w': _L0_ffn_in['gate_w'], 'L0_ffn_gate_b': _L0_ffn_in['gate_b'], 'L0_ffn_w1': _L0_ffn_in['w1'], 'L0_ffn_b1': _L0_ffn_in['b1'], 'L0_ffn_w2': _L0_ffn_in['w2'], 'L0_ffn_b2': _L0_ffn_in['b2']}

def reference(x, src, dst, edge_weight, L0_gnn_weight_l, L0_gnn_bias_l, L0_gnn_weight_r, L0_gnn_bias_r, L0_ffn_gate_w, L0_ffn_gate_b, L0_ffn_w1, L0_ffn_b1, L0_ffn_w2, L0_ffn_b2):
    import jax
    import jax.numpy as jnp

    def _L0_gnn_ref(x, edge_row, edge_col, edge_val, weight_l, bias_l, weight_r, bias_r):
        import jax, jax.numpy as jnp
        import numpy as np
        N = 3125
        E = 100000
        D_IN = 256
        D_OUT = 256
        h = x @ weight_l
        msgs = edge_val[:, None] * h[edge_col]
        agg = jax.ops.segment_sum(msgs, edge_row, num_segments=N)
        out = agg + bias_l
        out = out + x @ weight_r + bias_r
        return out

    def _L0_ffn_ref(h, gate_w, gate_b, w1, b1, w2, b2):
        import math
        import jax, jax.numpy as jnp
        import numpy as np
        CAPACITY_FACTOR = 1.25
        B, L, D = h.shape
        E = gate_w.shape[1]
        T = B * L
        C = max(1, math.ceil(CAPACITY_FACTOR * T / E))
        x = h.reshape(T, D)
        logits = x @ gate_w + gate_b
        probs = jax.nn.softmax(logits, axis=-1)
        idx = jnp.argmax(probs, axis=-1)
        prb = jnp.take_along_axis(probs, idx[:, None], axis=1)[:, 0]
        one_hot = jax.nn.one_hot(idx, E, dtype=jnp.float32)
        pos = (jnp.cumsum(one_hot, axis=0) * one_hot).sum(-1).astype(jnp.int32) - 1
        kept = pos < C
        pos_safe = jnp.where(kept, pos, C)
        buf = jnp.zeros((E, C, D), dtype=h.dtype).at[idx, pos_safe].set(x, mode='drop')
        hmid = jax.nn.relu(jnp.einsum('ecd,edf->ecf', buf, w1) + b1[:, None, :])
        ybuf = jnp.einsum('ecf,efd->ecd', hmid, w2) + b2[:, None, :]
        pos_g = jnp.minimum(pos, C - 1)
        y_tok = ybuf[idx, pos_g] * (prb * kept)[:, None]
        y = y_tok.reshape(B, L, D)
        y = jnp.nan_to_num(y, nan=0.0, posinf=10000.0, neginf=-10000.0)
        return y
    x = x + _L0_gnn_ref(_layernorm(x, axis=-1), src, dst, edge_weight, L0_gnn_weight_l, L0_gnn_bias_l, L0_gnn_weight_r, L0_gnn_bias_r)
    x = x + _L0_ffn_ref(_layernorm(x, axis=-1)[None], L0_ffn_gate_w, L0_ffn_gate_b, L0_ffn_w1, L0_ffn_b1, L0_ffn_w2, L0_ffn_b2)[0]
    return x

_drawn_inputs = setup_inputs


def setup_inputs(seed=0):
    import zlib

    import numpy as np

    out = dict(_drawn_inputs(seed))
    spreads = {'L0_ffn_gate_b': (0.0, 0.1), 'L0_ffn_b1': (0.0, 0.8), 'L0_ffn_b2': (0.0, 0.774)}
    factors = {}
    for name, (base, spread) in spreads.items():
        noise = np.random.default_rng([zlib.crc32(name.encode()), seed]).standard_normal(out[name].shape)
        drawn = base * np.exp(spread * noise) if base else spread * noise
        out[name] = jnp.asarray(drawn.astype(out[name].dtype))
    for name, factor in factors.items():
        out[name] = (out[name] * factor).astype(out[name].dtype)
    return out
```

```python
import concourse.bass as bass
from concourse import mybir
from contextlib import ExitStack

P = 128
N_NODES, D, F_HID, N_EXP = 3125, 256, 1024, 8
N_EDGES = 53125
KD = D // P
KF = F_HID // P
NB = -(-N_NODES // P)
LAST = N_NODES - (NB - 1) * P
EP = 125
EC = N_EDGES // EP
SC = 5
CC = EC // SC
UN = 5
NG = NB // UN
PIECE = CC // NG
CAP = 512
NJ = CAP // P
REC = 6
ROUNDS = -(-EP * CC // CAP)
LW = NB * REC
SLOTS = 489
ROWS_E = 512
NT = ROWS_E // P
ROW = 2 * D + 2
EPS = 1e-5
FLT_MAX = 3.4028234663852886e38
FAR = 65536.0
assert EP * EC == N_EDGES and SC * CC == EC and NG * PIECE == CC and NG * UN == NB


def graph_moe(nc, x, src, dst, edge_weight, weight_l, bias_l, weight_r, bias_r,
              gate_w, gate_b, w1, b1, w2, b2, h_rows, dispatch, out):
    f32, bf16, f16 = mybir.dt.float32, mybir.dt.bfloat16, mybir.dt.float16
    i32, u32 = mybir.dt.int32, mybir.dt.uint32
    ALU = mybir.AluOpType
    ACT = mybir.ActivationFunctionType
    AX = mybir.AxisListType
    ctx = ExitStack()

    def sb(name, shape, dt):
        return ctx.enter_context(nc.sbuf_tensor(name, shape, dt))

    def pb(name, shape, dt=f32):
        return ctx.enter_context(nc.psum_tensor(name, shape, dt))

    def sem(name):
        return ctx.enter_context(nc.semaphore(name))

    with ctx:
        ident = sb("ident", [P, P], f32)
        before = sb("before", [EP, EP], bf16)
        upto = sb("upto", [P, P], bf16)
        ones = sb("ones", [P, P], bf16)
        ones_row = sb("ones_row", [1, P], f32)
        run = sb("run", [EP, NB * CC], bf16)
        iota_block = sb("iota_block", [P, NB], f32)
        iota_node = sb("iota_node", [P, P], f32)
        iota_i = sb("iota_i", [P, CAP], i32)
        iota_rank = sb("iota_rank", [P, CAP], f16)
        rev = sb("rev", [P, N_EXP], f32)
        token1 = sb("token1", [P, NB], f32)
        valid = sb("valid", [P, NB], f32)
        fills = sb("fills", [P, 3, D], f32)
        zero_row = sb("zero_row", [P, ROW], f32)
        zero_bf = sb("zero_bf", [P, LW], bf16)
        wlr = sb("wlr", [P, KD, 2 * D], f32)
        bias = sb("bias", [P, 2, D], f32)
        gw = sb("gw", [P, KD, N_EXP], f32)
        gb = sb("gb", [1, N_EXP], f32)
        b1_rows = sb("b1_rows", [N_EXP * KF, P], f32)
        b1_cols = sb("b1_cols", [P, N_EXP * KF], f32)
        b2_all = sb("b2_all", [P, N_EXP, D], f32)
        w1_sb = sb("w1_sb", [P, 2, KD, F_HID], f32)
        w2_sb = sb("w2_sb", [P, 2, KF, D], f32)
        acc = sb("acc", [P, NB, D], f32)
        early = sb("early", [P, 2 * NB * D], f32)
        parts = {}

        def place(name, at, words, rows=P):
            parts[name] = (at, at + words)
            assert at + words <= 2 * NB * D
            return early[0:rows, at:at + words]

        x_sb = early[:, 0:NB * D].rearrange("p (n d) -> p n d", d=D)
        h_sb = early[:, NB * D:2 * NB * D].rearrange("p (n d) -> p n d", d=D)
        at_rank = place("at_rank", 0, PIECE * CAP // 2, EP).bitcast(bf16).rearrange("p (c r) -> p c r", c=PIECE)
        at_blk = place("at_blk", PIECE * CAP // 2, PIECE * LW // 2, EP).bitcast(bf16).rearrange(
            "p (c l) -> p c l", c=PIECE)
        hot = place("hot", NB * D, UN * NJ * P).rearrange("p (n m) -> p n m", m=P)
        drow = place("drow", NB * D + UN * NJ * P, UN * ROW).rearrange("p (u w) -> p u w", w=ROW)
        hid = place("hid", 0, 2 * KF * ROWS_E).rearrange("p (s f t) -> p s f t", s=2, f=KF)
        xnT = place("xnT", parts["hid"][1], 2 * KD * ROWS_E).rearrange("p (s k t) -> p s k t", s=2, k=KD)
        z_sb = place("z", parts["xnT"][1], NT * D).rearrange("p (t d) -> p t d", d=D)
        odd = place("odd", parts["z"][1], 3 * D).bitcast(i32).rearrange("p (i d) -> p i d", i=3)
        stats = sb("stats", [P, UN, 6], f32)
        moments = sb("moments", [P, UN, 2], f32)
        rstd = sb("rstd", [P, UN, 1], f32)
        xn = sb("xn", [P, UN, D], f32)
        xt = sb("xt", [P, UN, D], f32)
        e_src = sb("e_src", [EP, EC], i32)
        e_dst = sb("e_dst", [EP, EC], i32)
        e_w = sb("e_w", [EP, EC], f32)
        landed = sb("landed", [P, max(UN * NJ * D, 2 * NT * ROW)], f32)
        fetched = landed[:, 0:UN * NJ * D].rearrange("p (n d) -> p n d", d=D)
        e_bits = landed[0:EP, 0:4 * EC].bitcast(i32).rearrange("p (i c) -> p i c", i=4)
        w_rest = landed[0:EP, 4 * EC:5 * EC]
        rank_top = sb("rank_top", [EP, 1], f32)
        rank_max = sb("rank_max", [1, 1], i32)
        blk = sb("blk", [EP, EC], f32)
        rec = sb("rec", [EP, EC, REC], bf16)
        in_blk = sb("in_blk", [EP, NB * CC], bf16)
        count = sb("count", [EP, NB * CC], f32)
        total = sb("total", [EP, NB], bf16)
        rank = sb("rank", [EP, EC], f32)
        t_dst = sb("t_dst", [P, (SC + 1) * NB * NJ], u32)
        tmp_dst = sb("tmp_dst", [P, NJ, NB], f32)
        t_src = sb("t_src", [P, (SC + 1) * NB * NJ], f32)
        t_w = sb("t_w", [P, (SC + 1) * NB * NJ], f32)
        idx = sb("idx", [P, UN, NJ], u32)
        sm = sb("sm", [P, 8, UN, N_EXP], f32)
        sc1 = sb("sc1", [P, 8, UN], f32)
        hot_e = sb("hot_e", [P, UN, N_EXP], bf16)
        hot_sum = sb("hot_sum", [P, N_EXP], bf16)
        hot_new = sb("hot_new", [P, N_EXP], f32)
        slot = sb("slot", [P, UN], u32)
        xs = landed[:, 0:2 * NT * ROW].rearrange("p (s t w) -> p s t w", s=2, t=NT)
        tok = sb("tok", [P, 2, NT], u32)
        tok_f = sb("tok_f", [P, 2, NT], f32)

        bank = [pb(f"bank{i}", [P, 512]) for i in range(4, 8)]
        ps_sort = pb("ps_sort", [P, 4, 512])

        def b(i):
            return ps_sort[:, i, :] if i < 4 else bank[i - 4][:, :]

        TP, HL, HR = (0, 1, 0, 1, 0), (2, 3, 4, 2, 3), (5, 6, 7, 5, 6)
        AG = (4, 5, 6, 4, 5)
        UP, DOWN = (2, 3, 4, 2, 3, 4, 2, 3), (5, 6, 7, 5)

        LG = b(2)[:, 0:UN * N_EXP].rearrange("p (u e) -> p u e", e=N_EXP)
        POS = b(3)[:, 0:UN * N_EXP].rearrange("p (u e) -> p u e", e=N_EXP)

        def used(banks, u):
            n = len(banks)
            return next(v for v in range(n + u - 1, -1, -1) if banks[v % n] == banks[u]) + 1

        names = ("const passed consts2 edges_in w_in x_in bits_ready parts_ready wparts_ready total_ready base_ready "
                 "var_ready std_ready xn_ready tp_ready xt_ready hp_ready h_evac acc_init acc0 h_ready h_stored "
                 "blk_ready rank_ready sort_used sort_done table_ready idx_ready hot_ready agg_done "
                 "acc_added zeroed x2_ready x1_copied tp2_ready xt2_ready lg_ready lmax_ready exp_ready "
                 "hote_ready pos_ready slot_ready drow_free dispatched x1_out "
                 "xs_free tpe_ready xte_ready hl_ready relu_done y_ready y_read z_ready z_free b1_in b1_t b1_ready "
                 "top_ready top_t max_ready").split()
        S = {n: sem(n) for n in names}
        S["fetch"] = [sem(f"fetch{u}") for u in range(UN)]
        R = {n: sem("more_" + n) for n in ("rank_ready sort_used sort_done table_ready idx_ready hot_ready "
                                           "agg_done acc_added swept").split()}
        R["fetch"] = [sem(f"more_fetch{u}") for u in range(UN)]
        s_disp = [sem(f"disp{u}") for u in range(UN)]
        s_w = [sem(f"w_expert{i}") for i in range(2)]
        s_xs = [sem(f"xs_in{i}") for i in range(2)]
        s_out = [sem(f"out_tile{t}") for t in range(NT)]

        def after(eng, semaphore, value):
            eng.wait_ge(semaphore, value)
            eng.sem_inc(S["passed"], 1)

        def more_rounds(eng, free, body):
            eng.wait_ge(S["max_ready"], 1)
            largest = eng.value_load(rank_max[0:1, 0:1], min_val=0, max_val=EP * CC)
            with eng.If(largest > CAP):
                for name, n in free:
                    eng.sem_inc(R[name], n)
                with eng.Fori(1, ROUNDS) as r:
                    with eng.If(largest > r * CAP):
                        with eng.Fori(0, SC) as s:
                            k = (r - 1) * SC + s
                            body(s, k)
                            eng.wait_ge(R["swept"], k + 1)
                            eng.sem_inc(S["passed"], 1)

        block = ctx.enter_context(nc.Block())

        @block.sync
        def _(sp):
            e_view = "(p c) -> p c"
            sp.dma_start(e_src[:, :], src.rearrange(e_view, c=EC)).then_inc(S["edges_in"], 16)
            sp.dma_start(e_dst[:, :], dst.rearrange(e_view, c=EC)).then_inc(S["edges_in"], 16)
            sp.dma_start(e_w[:, :], edge_weight.rearrange(e_view, c=EC)).then_inc(S["edges_in"], 16)
            sp.wait_ge(S["consts2"], 1)
            sp.dma_start(x_sb[:, 0:NB - 1, :], x[0:(NB - 1) * P, :].rearrange("(n p) d -> p n d", p=P)
                         ).then_inc(S["x_in"], 16)
            sp.dma_start(x_sb[0:LAST, NB - 1, :], x[(NB - 1) * P:N_NODES, :]).then_inc(S["x_in"], 16)
            with sp.Fori(0, NG) as g:
                sp.wait_ge(S["h_evac"], g * UN + 2 * UN)
                sp.dma_start(h_rows[bass.ds(g * (UN * P), UN * P), :].rearrange("(n p) d -> p n d", p=P),
                             h_sb[:, bass.ds(g * UN, UN), :]).then_inc(S["h_stored"], 16)
            for e in range(2):
                sp.dma_start(w1_sb[:, e, :, :], w1[e].rearrange("(k p) f -> p k f", p=P)).then_inc(s_w[e], 16)
                sp.dma_start(w2_sb[:, e, :, :], w2[e].rearrange("(f p) d -> p f d", p=P)).then_inc(s_w[e], 16)
            sp.wait_ge(S["zeroed"], 1)
            sp.dma_start(dispatch.rearrange("(n p) w -> p n w", p=P),
                         zero_row[:, None, :].broadcast_to([P, N_EXP * NT, ROW])).then_inc(S["dispatched"], 16)
            sp.wait_ge(S["acc_added"], SC * NB + UN)
            sp.dma_start(out[0:(NB - 1) * P, :].rearrange("(n p) d -> p n d", p=P), acc[:, 0:NB - 1, :]
                         ).then_inc(S["x1_out"], 16)
            sp.dma_start(out[(NB - 1) * P:N_NODES, :], acc[0:LAST, NB - 1, :]).then_inc(S["x1_out"], 16)

            def load_rows(e, s):
                sp.wait_ge(S["xs_free"], e + 1)
                sp.dma_start(xs[:, s, :, :], dispatch[bass.ds(e * ROWS_E, ROWS_E), :].rearrange(
                    "(t p) w -> p t w", p=P)).then_inc(s_xs[s], 16)

            sp.wait_ge(S["drow_free"], NG + 1)
            load_rows(0, 0)
            with sp.Fori(0, (N_EXP - 2) // 2) as q:
                for s in range(2):
                    load_rows(2 * q + (s + 1), 1 - s)
                    sp.wait_ge(S["y_ready"], 8 * q + 4 * (s + 1))
                    e2 = 2 * q + (s + 2)
                    sp.dma_start(w1_sb[:, s, :, :], w1[bass.ds(e2, 1)].rearrange("a (k p) f -> p (a k) f", p=P)
                                 ).then_inc(s_w[s], 16)
                    sp.dma_start(w2_sb[:, s, :, :], w2[bass.ds(e2, 1)].rearrange("a (f p) d -> p (a f) d", p=P)
                                 ).then_inc(s_w[s], 16)
            load_rows(N_EXP - 1, 1)

        @block.gpsimd
        def _(pool):
            pool.memset(x_sb[:, NB - 1, :], 0.0).then_inc(S["consts2"], 1)
            pool.memset(ident[:, :], 0.0)
            pool.memset(before[:, :], 1.0)
            pool.memset(upto[:, :], 1.0)
            pool.iota(iota_block[:, :], pattern=[[1, NB]], base=0, channel_multiplier=0,
                      allow_small_or_imprecise_dtypes=True)
            pool.iota(iota_node[:, :], pattern=[[1, P]], base=0, channel_multiplier=0,
                      allow_small_or_imprecise_dtypes=True)
            pool.iota(iota_i[:, :], pattern=[[1, CAP]], base=1, channel_multiplier=0)
            pool.iota(rev[:, :], pattern=[[-1, N_EXP]], base=N_EXP, channel_multiplier=0,
                      allow_small_or_imprecise_dtypes=True)
            pool.iota(token1[:, :], pattern=[[P, NB]], base=1, channel_multiplier=1,
                      allow_small_or_imprecise_dtypes=True)
            pool.memset(ones[:, :], 1.0)
            pool.memset(ones_row[:, :], 1.0)
            pool.memset(run[:, :], 1.0)
            pool.memset(fills[:, 0, :], 0.0)
            pool.memset(fills[:, 1, :], 1e4)
            pool.memset(fills[:, 2, :], -1e4)
            pool.memset(hot_sum[:, :], 0.0)
            pool.drain()
            pool.memset(run[:, :].rearrange("p (b c) -> p b c", c=CC)[:, :, 0:1], 0.0)
            pool.affine_select(out=ident[:, :], in_=ident[:, :], compare_op=ALU.not_equal, fill=1.0,
                               base=0, pattern=[[-1, P]], channel_multiplier=1)
            pool.affine_select(out=before[:, :], in_=before[:, :], compare_op=ALU.is_gt, fill=0.0,
                               base=0, pattern=[[1, EP]], channel_multiplier=-1)
            pool.affine_select(out=upto[:, :], in_=upto[:, :], compare_op=ALU.is_ge, fill=0.0,
                               base=0, pattern=[[1, P]], channel_multiplier=-1)
            pool.drain()
            pool.memset(zero_row[:, :], 0.0).then_inc(S["zeroed"], 1)
            pool.drain()
            pool.sem_inc(S["const"], 1)
            pool.wait_ge(S["edges_in"], 48)
            pool.tensor_copy(rec[:, :, 3], e_w[:, :])
            pool.drain()
            pool.tensor_tensor(w_rest, e_w[:, :], rec[:, :, 3], ALU.subtract)
            pool.drain()
            pool.tensor_copy(rec[:, :, 4], w_rest)
            pool.drain()
            pool.tensor_tensor(rec[:, :, 5], w_rest, rec[:, :, 4], ALU.subtract
                               ).then_inc(S["wparts_ready"], 1)
            pool.wait_ge(S["w_in"], 96)
            pool.wait_ge(S["x_in"], 32)
            pool.tensor_tensor(bias[:, 0, :], bias[:, 0, :], bias[:, 1, :], ALU.add)
            pool.drain()
            with pool.Fori(0, NB) as t:
                pool.tensor_tensor(acc[:, t, :], x_sb[:, t, :], bias[:, 0, :], ALU.add
                                   ).then_inc(S["acc_init"], 1)

            def gathers(Q, n):
                for u in range(UN):
                    after(pool, Q["idx_ready"], n * UN + (u + 1))
                    for j in range(NJ):
                        pool.indirect_dma_start(
                            fetched[:, u * NJ + j, :], None, h_rows,
                            bass.IndirectOffsetOnAxis(ap=idx[:, u, j:j + 1], axis=0)).then_inc(Q["fetch"][u], 16)

            def scatters(g):
                for u in range(UN):
                    after(pool, S["slot_ready"], g + 1)
                    pool.indirect_dma_start(
                        dispatch, bass.IndirectOffsetOnAxis(ap=slot[:, u:u + 1], axis=0), drow[:, u, :], None,
                        bounds_check=N_EXP * ROWS_E - 1, oob_is_err=False).then_inc(s_disp[u], 16)
                for u in range(UN):
                    after(pool, s_disp[u], (g + 1) * 16)
                pool.sem_inc(S["drow_free"], 1)

            pool.wait_ge(S["h_stored"], NG * 16)
            with pool.Fori(0, (SC - 1) * NG) as n:
                gathers(S, n)

            def more(s, k):
                with pool.Fori(0, NG) as g:
                    gathers(R, k * NG + g)

            more_rounds(pool, (), more)
            gathers(S, (SC - 1) * NG)
            pool.wait_ge(S["dispatched"], 16)
            with pool.Fori(0, NG - 1) as g:
                gathers(S, g + ((SC - 1) * NG + 1))
                scatters(g)
            scatters(NG - 1)
            pool.wait_ge(S["x1_out"], 32)
            with pool.Fori(0, N_EXP // 2) as q:
                for s in range(2):
                    for t in range(NT):
                        rows = P if t < NT - 1 else SLOTS - (NT - 1) * P
                        after(pool, S["z_ready"], 8 * q + (4 * s + t + 1))
                        pool.indirect_dma_start(
                            out, bass.IndirectOffsetOnAxis(ap=tok[0:rows, s, t:t + 1], axis=0),
                            z_sb[0:rows, t, :], None,
                            bounds_check=N_NODES - 1, oob_is_err=False).then_inc(s_out[t], 16)
                    for t in range(NT):
                        after(pool, s_out[t], 32 * q + 16 * (s + 1))
                    pool.sem_inc(S["z_free"], 1)

        @block.scalar
        def _(act):
            for k in range(KD):
                act.dma_start(wlr[:, k, 0:D], weight_l[k * P:(k + 1) * P, :]).then_inc(S["w_in"], 16)
                act.dma_start(wlr[:, k, D:2 * D], weight_r[k * P:(k + 1) * P, :]).then_inc(S["w_in"], 16)
            act.dma_start(bias[:, 0, :], bias_l[None, :].broadcast_to([P, D])).then_inc(S["w_in"], 16)
            act.dma_start(bias[:, 1, :], bias_r[None, :].broadcast_to([P, D])).then_inc(S["w_in"], 16)
            act.dma_start(gw[:, :, :], gate_w.rearrange("(k p) e -> p k e", p=P)).then_inc(S["b1_in"], 16)
            act.dma_start(gb[:, :], gate_b[None, :]).then_inc(S["b1_in"], 16)
            act.dma_start(b1_rows[:, :], b1.rearrange("e (f p) -> (e f) p", p=P)).then_inc(S["b1_in"], 16)
            act.dma_start(b2_all[:, :, :].rearrange("p e d -> p (e d)"),
                          b2.rearrange("e d -> (e d)")[None, :].broadcast_to([P, N_EXP * D])
                          ).then_inc(S["b1_in"], 16)
            act.sem_inc(S["xt_ready"], UN)
            act.sem_inc(S["h_evac"], UN)
            act.wait_ge(S["bits_ready"], 1)
            act.activation(blk[:, :], e_bits[:, 0, :], ACT.Copy)
            for i in range(3):
                last = act.activation(rec[:, :, i], e_bits[:, i + 1, :], ACT.Copy)
            act.drain()
            act.sem_inc(S["parts_ready"], 1)
            act.wait_ge(S["b1_t"], 1)
            act.activation(b1_cols[:, :], b(7)[:, 0:N_EXP * KF], ACT.Copy).then_inc(S["b1_ready"], 1)
            def root(i):
                act.wait_ge(S["var_ready"], i + 1)
                act.activation(rstd[:, :, :], rstd[:, :, :], ACT.Sqrt).then_inc(S["std_ready"], 1)

            def turned_out(g):
                for u in range(UN):
                    act.wait_ge(S["tp_ready"], g * UN + (UN + u + 1))
                    act.wait_ge(S["hp_ready"], g * UN + (u + 1))
                    act.activation(xt[:, u, :], b(TP[u])[:, 0:D], ACT.Copy).then_inc(S["xt_ready"], 1)

            def h_out(g):
                for u in range(UN):
                    act.wait_ge(S["hp_ready"], g * UN + (UN + u + 1))
                    act.activation(h_sb[:, g * UN + u, :], b(HL[u])[:, 0:D], ACT.Copy
                                   ).then_inc(S["h_evac"], 1)

            root(0)
            with act.Fori(0, NG - 1) as g:
                turned_out(g)
                root(g + 1)
                h_out(g)
            turned_out(NG - 1)
            h_out(NG - 1)

            def copy_idx(Q, at, n, u):
                act.wait_ge(Q["agg_done"], n * UN + (u + 1))
                act.activation(idx[:, u, :], t_dst[:, bass.ds(at * (UN * NJ) + u * NJ, NJ)], ACT.Copy
                               ).then_inc(Q["idx_ready"], 1)

            with act.Fori(0, SC - 1) as s:
                act.wait_ge(S["table_ready"], s + 1)
                with act.Fori(0, NG) as g:
                    for u in range(UN):
                        copy_idx(S, s * NG + g, s * NG + g, u)

            def route(g):
                act.wait_ge(S["drow_free"], g + 1)
                for u in range(UN):
                    act.wait_ge(S["acc_added"], g * UN + ((SC - 1) * NB + UN + u + 1))
                    act.activation(drow[:, u, 0:D], acc[:, g * UN + u, :], ACT.Copy).then_inc(S["x1_copied"], 1)
                root(g + NG)
                for u in range(UN):
                    act.wait_ge(S["tp2_ready"], g * UN + (u + 1))
                    act.wait_ge(S["lg_ready"], g + 1)
                    act.activation(xt[:, u, :], b(TP[u])[:, 0:D], ACT.Copy).then_inc(S["xt2_ready"], 1)
                act.wait_ge(S["lmax_ready"], g + 1)
                act.activation(sm[:, 1, :, :], sm[:, 0, :, :], ACT.Exp).then_inc(S["exp_ready"], 1)

            def more(s, k):
                act.wait_ge(R["table_ready"], k + 1)
                with act.Fori(0, NG) as g:
                    for u in range(UN):
                        copy_idx(R, g + SC * NG, k * NG + g, u)

            more_rounds(act, (), more)
            for u in range(UN):
                copy_idx(S, (SC - 1) * NG, (SC - 1) * NG, u)
            with act.Fori(0, NG - 1) as g:
                for u in range(UN):
                    copy_idx(S, g + ((SC - 1) * NG + 1), g + ((SC - 1) * NG + 1), u)
                route(g)
            route(NG - 1)

            act.wait_ge(S["b1_ready"], 1)
            with act.Fori(0, N_EXP // 2) as q:
                for s in range(2):
                    for k in range(KD):
                        act.wait_ge(S["tpe_ready"], 4 * q + (2 * s + k + 1))
                        act.activation(xnT[:, s, k, :], b(k), ACT.Copy).then_inc(S["xte_ready"], 1)
                    for f in range(KF):
                        act.wait_ge(S["hl_ready"], 16 * q + (8 * s + f + 1))
                        act.activation(hid[:, s, f, 0:SLOTS], b(UP[f])[:, 0:SLOTS], ACT.Relu,
                                       bias=b1_cols[:, bass.ds(16 * q + (8 * s + f), 1)]
                                       ).then_inc(S["relu_done"], 1)

        @block.tensor
        def _(pe):
            pe.sem_inc(S["agg_done"], UN)
            pe.sem_inc(S["tp_ready"], UN)
            pe.sem_inc(S["hp_ready"], UN)
            pe.sem_inc(S["sort_used"], 1)
            pe.sem_inc(S["lg_ready"], 1)
            pe.wait_ge(S["const"], 1)
            pe.wait_ge(S["b1_in"], 64)
            pe.transpose(b(7)[:, 0:N_EXP * KF], b1_rows[:, :], ident[0:N_EXP * KF, 0:N_EXP * KF]
                         ).then_inc(S["b1_t"], 1)
            pe.wait_ge(S["w_in"], 96)
            pe.wait_ge(S["b1_ready"], 1)

            with pe.Fori(0, NG) as g:
                for u in range(UN):
                    pe.wait_ge(S["xn_ready"], g * UN + (u + 1))
                    pe.wait_ge(S["xt_ready"], g * UN + used(TP, u))
                    for k in range(KD):
                        last = pe.transpose(b(TP[u])[:, k * P:(k + 1) * P], xn[:, u, k * P:(k + 1) * P], ident[:, :])
                    last.then_inc(S["tp_ready"], 1)
                for u in range(UN):
                    pe.wait_ge(S["xt_ready"], g * UN + (UN + u + 1))
                    pe.wait_ge(S["h_evac"], g * UN + used(HL, u))
                    pe.wait_ge(S["acc0"], g * UN + used(HR, u))
                    for side, banks in enumerate((HL, HR)):
                        for k in range(KD):
                            last = pe.matmul(b(banks[u])[:, 0:D], lhsT=xt[:, u, k * P:(k + 1) * P],
                                             rhs=wlr[:, k, side * D:(side + 1) * D],
                                             start=(k == 0), stop=(k == KD - 1))
                    last.then_inc(S["hp_ready"], 1)

            def base(s):
                pe.wait_ge(S["total_ready"], s + 1)
                pe.matmul(b(7)[0:EP, 0:NB], lhsT=before[:, :], rhs=total[:, :], start=True, stop=True
                          ).then_inc(S["base_ready"], 1)

            def open_sort():
                for j in range(NJ):
                    pe.matmul(ps_sort[:, j, 0:LW], lhsT=zero_bf[0:EP, 0:P], rhs=zero_bf[0:EP, 0:LW],
                              start=True, stop=False)

            def close_sort(Q):
                for j in range(NJ):
                    last = pe.matmul(ps_sort[:, j, 0:LW], lhsT=zero_bf[0:EP, 0:P], rhs=zero_bf[0:EP, 0:LW],
                                     start=False, stop=True)
                last.then_inc(Q["sort_done"], 1)

            def sort_piece(Q, m):
                for c in range(PIECE):
                    pe.wait_ge(Q["rank_ready"], m * PIECE + (c + 1))
                    for j in range(NJ):
                        last = pe.matmul(ps_sort[:, j, 0:LW], lhsT=at_rank[:, c, j * P:(j + 1) * P],
                                         rhs=at_blk[:, c, :], start=False, stop=False)
                last.then_inc(Q["sort_used"], 1)

            def aggregate(Q, n):
                for u in range(UN):
                    pe.wait_ge(Q["fetch"][u], n * (16 * NJ) + 16 * NJ)
                    pe.wait_ge(Q["hot_ready"], n * (UN * NJ) + (u + 1) * NJ)
                    pe.wait_ge(Q["acc_added"], n * UN + used(AG, u))
                    for j in range(NJ):
                        last = pe.matmul(b(AG[u])[:, 0:D], lhsT=hot[:, u * NJ + j, :], rhs=fetched[:, u * NJ + j, :],
                                         start=(j == 0), stop=(j == NJ - 1))
                    last.then_inc(Q["agg_done"], 1)

            base(0)
            pe.wait_ge(S["h_evac"], NB + UN)
            open_sort()
            with pe.Fori(0, NG) as g:
                sort_piece(S, g)
            close_sort(S)
            pe.wait_ge(S["acc0"], NB + UN)
            with pe.Fori(0, SC - 1) as s:
                base(s + 1)
                pe.wait_ge(S["table_ready"], s + 1)
                open_sort()
                with pe.Fori(0, NG) as g:
                    aggregate(S, s * NG + g)
                    sort_piece(S, (s + 1) * NG + g)
                close_sort(S)

            def route(g):
                for u in range(UN):
                    pe.wait_ge(S["x2_ready"], g * UN + (u + 1))
                    pe.wait_ge(S["xt2_ready"], g * UN + used(TP, u))
                    for k in range(KD):
                        last = pe.transpose(b(TP[u])[:, k * P:(k + 1) * P],
                                            drow[:, u, D + k * P:D + (k + 1) * P], ident[:, :])
                    last.then_inc(S["tp2_ready"], 1)
                for u in range(UN):
                    pe.wait_ge(S["xt2_ready"], g * UN + (UN + u + 1))
                    for k in range(KD):
                        pe.matmul(LG[:, u, :], lhsT=xt[:, u, k * P:(k + 1) * P], rhs=gw[:, k, :],
                                  start=(k == 0), stop=False)
                    last = pe.matmul(LG[:, u, :], lhsT=ones_row[:, :], rhs=gb[:, :], start=False, stop=True)
                last.then_inc(S["lg_ready"], 1)
                pe.wait_ge(S["hote_ready"], g + 1)
                for u in range(UN):
                    pe.matmul(POS[:, u, :], lhsT=ones[:, :], rhs=hot_sum[:, :], start=True, stop=False)
                    for v in range(u):
                        pe.matmul(POS[:, u, :], lhsT=ones[:, :], rhs=hot_e[:, v, :], start=False, stop=False)
                    last = pe.matmul(POS[:, u, :], lhsT=upto[:, :], rhs=hot_e[:, u, :], start=False, stop=True)
                last.then_inc(S["pos_ready"], 1)

            pe.wait_ge(S["top_ready"], 1)
            pe.transpose(b(7)[0:1, 0:EP], rank_top[:, :], ident[0:EP, 0:EP]).then_inc(S["top_t"], 1)

            def more(s, k):
                open_sort()
                with pe.Fori(0, NG) as g:
                    sort_piece(R, k * NG + g)
                close_sort(R)
                with pe.Fori(0, NG) as g:
                    aggregate(R, k * NG + g)

            more_rounds(pe, (("agg_done", UN), ("sort_used", 1)), more)
            with pe.Fori(0, NG) as g:
                aggregate(S, g + (SC - 1) * NG)
                route(g)

            def turn_rows(e, s):
                pe.wait_ge(s_xs[s], 8 * (e - s) + 16)
                pe.wait_ge(S["xte_ready"], 2 * e + 2)
                for k in range(KD):
                    for t in range(NT):
                        last = pe.transpose(b(k)[:, t * P:(t + 1) * P], xs[:, s, t, D + k * P:D + (k + 1) * P],
                                            ident[:, :])
                    last.then_inc(S["tpe_ready"], 1)

            def up(e, s):
                pe.wait_ge(s_w[s], 16 * (e - s) + 32)
                pe.wait_ge(S["xte_ready"], 2 * e + 4)
                for f in range(KF):
                    pe.wait_ge(S["relu_done"], 8 * e + used(UP, f))
                    for k in range(KD):
                        last = pe.matmul(b(UP[f])[:, 0:SLOTS], lhsT=w1_sb[:, s, k, f * P:(f + 1) * P],
                                         rhs=xnT[:, s, k, 0:SLOTS], start=(k == 0), stop=(k == KD - 1))
                    last.then_inc(S["hl_ready"], 1)

            def down(e, s):
                pe.wait_ge(S["relu_done"], 8 * e + 2 * KF)
                for t in range(NT):
                    rows = P if t < NT - 1 else SLOTS - (NT - 1) * P
                    pe.wait_ge(S["y_read"], 4 * e + used(DOWN, t))
                    for f in range(KF):
                        last = pe.matmul(b(DOWN[t])[0:rows, 0:D], lhsT=hid[:, s, f, t * P:t * P + rows],
                                         rhs=w2_sb[:, s, f, :], start=(f == 0), stop=(f == KF - 1))
                    last.then_inc(S["y_ready"], 1)

            turn_rows(0, 0)
            up(0, 0)
            with pe.Fori(0, (N_EXP - 2) // 2) as q:
                turn_rows(2 * q + 1, 1)
                down(2 * q, 0)
                up(2 * q + 1, 1)
                turn_rows(2 * q + 2, 0)
                down(2 * q + 1, 1)
                up(2 * q + 2, 0)
            turn_rows(N_EXP - 1, 1)
            down(N_EXP - 2, 0)
            up(N_EXP - 1, 1)
            down(N_EXP - 1, 1)

        @block.vector
        def _(dve):
            dve.sem_inc(S["acc0"], UN)
            dve.sem_inc(S["acc_added"], UN)
            dve.sem_inc(S["xt2_ready"], UN)
            dve.sem_inc(S["xte_ready"], 2)
            dve.sem_inc(S["relu_done"], KF)
            dve.sem_inc(S["y_read"], NT)
            dve.sem_inc(S["xs_free"], 2)
            dve.sem_inc(S["z_free"], 1)
            dve.sem_inc(S["drow_free"], 1)
            dve.memset(zero_bf[:, :], 0.0)
            dve.wait_ge(S["edges_in"], 48)
            for i, (data, op, by) in enumerate(((e_src, ALU.logical_shift_right, 7), (e_src, ALU.bitwise_and, 127),
                                                (e_dst, ALU.logical_shift_right, 4), (e_dst, ALU.bitwise_and, 15))):
                last = dve.tensor_scalar(e_bits[:, i, :], data[:, :], by, None, op)
            last.then_inc(S["bits_ready"], 1)
            dve.wait_ge(S["const"], 1)
            dve.tensor_copy(iota_rank[:, :], iota_i[:, :])
            dve.tensor_scalar(valid[:, :], token1[:, :], float(N_NODES), None, ALU.is_le)

            blkT = in_blk[:, :].rearrange("p (b c) -> p b c", c=CC)
            countT = count[:, :].rearrange("p (b c) -> p b c", c=CC)

            def block_hot(s):
                dve.tensor_tensor(blkT, blk[:, None, bass.ds(s * CC, CC)].broadcast_to([EP, NB, CC]),
                                  iota_block[0:EP, :, None].broadcast_to([EP, NB, CC]), ALU.is_equal)
                dve.drain()

            def ranks(s):
                if isinstance(s, int):
                    dve.wait_ge(S["parts_ready"], 1)
                block_hot(s)
                dve.tensor_tensor_scan(count[:, :], run[:, :], in_blk[:, :], 0.0, ALU.mult, ALU.add)
                dve.drain()
                dve.tensor_copy(total[:, :], countT[:, :, CC - 1]).then_inc(S["total_ready"], 1)
                dve.wait_ge(S["base_ready"], s + 1)
                dve.tensor_tensor(countT, countT, b(7)[0:EP, 0:NB, None].broadcast_to([EP, NB, CC]), ALU.add)
                dve.drain()
                dve.tensor_tensor(count[:, :], count[:, :], in_blk[:, :], ALU.mult)
                dve.drain()
                dve.tensor_reduce(rank[:, bass.ds(s * CC, CC)], count[:, :].rearrange("p (b c) -> p c b", c=CC),
                                  AX.X, ALU.add)
                dve.drain()

            def build_piece(Q, s, g, m):
                c0 = s * CC + g * PIECE
                dve.wait_ge(Q["sort_used"], m + 1)
                dve.tensor_tensor(at_blk[:, :, :].rearrange("p c (b i) -> p c b i", i=REC),
                                  in_blk[:, :].rearrange("p (b c) -> p c b", c=CC)[:, bass.ds(g * PIECE, PIECE), :, None]
                                  .broadcast_to([EP, PIECE, NB, REC]),
                                  rec[:, bass.ds(c0, PIECE), None, :].broadcast_to([EP, PIECE, NB, REC]), ALU.mult)
                dve.drain()
                for c in range(PIECE):
                    dve.tensor_scalar(at_rank[:, c, :], iota_rank[0:EP, :], rank[:, bass.ds(c0 + c, 1)], None,
                                      ALU.is_equal).then_inc(Q["rank_ready"], 1)

            def take_table(Q, at, k):
                dve.wait_ge(Q["sort_done"], k + 1)

                def part(i):
                    return ps_sort[:, 0:NJ, 0:LW].rearrange("p j (b i) -> p j b i", i=REC)[:, :, :, i]

                def table(t):
                    return t[:, bass.ds(at * (NB * NJ), NB * NJ)].rearrange("p (b j) -> p j b", j=NJ)

                dve.tensor_copy(table(t_src), part(0))
                dve.tensor_copy(table(t_w), part(3))
                dve.tensor_scalar(tmp_dst[:, :, :], part(1), 16.0, None, ALU.mult)
                dve.drain()
                dve.tensor_tensor(table(t_w), table(t_w), part(4), ALU.add)
                dve.tensor_tensor(table(t_dst), tmp_dst[:, :, :], part(2), ALU.add)
                dve.drain()
                dve.tensor_tensor(table(t_w), table(t_w), part(5), ALU.add)
                dve.drain()
                dve.sem_inc(Q["table_ready"], 1)

            def weighted_hot(Q, at_n, n):
                for u in range(UN):
                    dve.wait_ge(Q["agg_done"], n * UN + (u + 1))
                    for j in range(NJ):
                        at = at_n * (UN * NJ) + (u * NJ + j)
                        dve.tensor_scalar(hot[:, u * NJ + j, :], iota_node[:, :], t_src[:, bass.ds(at, 1)],
                                          t_w[:, bass.ds(at, 1)], ALU.is_equal, ALU.mult
                                          ).then_inc(Q["hot_ready"], 1)

            def add_blocks(Q, n, g):
                for u in range(UN):
                    dve.wait_ge(Q["agg_done"], n * UN + (UN + u + 1))
                    dve.tensor_tensor(acc[:, g * UN + u, :], acc[:, g * UN + u, :], b(AG[u])[:, 0:D], ALU.add
                                      ).then_inc(Q["acc_added"], 1)

            def layernorm(i, rows, outs, ready):
                for u in range(UN):
                    dve.bn_stats(stats[:, u, :], rows(u))
                dve.drain()
                for u in range(UN):
                    dve.bn_aggr(moments[:, u, :], stats[:, u, :])
                dve.drain()
                dve.tensor_scalar(rstd[:, :, :], moments[:, :, 1:2], EPS, None, ALU.add).then_inc(S["var_ready"], 1)
                dve.wait_ge(S["std_ready"], i + 1)
                dve.reciprocal(rstd[:, :, :], rstd[:, :, :])
                dve.drain()
                for u in range(UN):
                    dve.tensor_scalar(outs(u), rows(u), moments[:, u, 0:1], rstd[:, u, :],
                                      ALU.subtract, ALU.mult).then_inc(ready, 1)

            def first_norm(g):
                after(dve, S["tp_ready"], g * UN + UN)
                layernorm(g, lambda u: x_sb[:, g * UN + u, :], lambda u: xn[:, u, :], S["xn_ready"])

            def first_add(g):
                for u in range(UN):
                    dve.wait_ge(S["hp_ready"], g * UN + (UN + u + 1))
                    dve.wait_ge(S["acc_init"], g * UN + (u + 1))
                    dve.tensor_tensor(acc[:, g * UN + u, :], acc[:, g * UN + u, :], b(HR[u])[:, 0:D],
                                      ALU.add).then_inc(S["acc0"], 1)

            dve.wait_ge(S["x_in"], 32)
            first_norm(0)
            with dve.Fori(0, NG - 1) as g:
                first_norm(g + 1)
                first_add(g)
            first_add(NG - 1)
            dve.drain()

            ranks(0)
            dve.wait_ge(S["wparts_ready"], 1)
            dve.wait_ge(S["h_stored"], NG * 16)
            with dve.Fori(0, NG) as g:
                build_piece(S, 0, g, g)
            take_table(S, 0, 0)
            with dve.Fori(0, SC - 1) as s:
                ranks(s + 1)
                with dve.Fori(0, NG) as g:
                    weighted_hot(S, s * NG + g, s * NG + g)
                    build_piece(S, s + 1, g, (s + 1) * NG + g)
                    add_blocks(S, s * NG + g, g)
                take_table(S, s + 1, s + 1)

            dve.tensor_reduce(rank_top[:, :], rank[:, :], AX.X, ALU.max).then_inc(S["top_ready"], 1)
            dve.wait_ge(S["top_t"], 1)
            dve.tensor_reduce(rank_max[:, :], b(7)[0:1, 0:EP], AX.X, ALU.max).then_inc(S["max_ready"], 1)

            def more(s, k):
                with dve.If(s == 0):
                    dve.tensor_scalar(rank[:, :], rank[:, :], float(-CAP), None, ALU.add)
                    dve.drain()
                block_hot(s)
                with dve.Fori(0, NG) as g:
                    build_piece(R, s, g, k * NG + g)
                take_table(R, SC, k)
                with dve.Fori(0, NG) as g:
                    weighted_hot(R, g + SC * NG, k * NG + g)
                    add_blocks(R, k * NG + g, g)
                dve.drain()
                dve.sem_inc(R["swept"], 1)

            more_rounds(dve, (("acc_added", UN),), more)

            def smv(i):
                return sm[:, i, :, :]

            def wide(ap):
                return ap[:, :, None].broadcast_to([P, UN, N_EXP])

            rev5 = rev[:, None, :].broadcast_to([P, UN, N_EXP])
            MAXL, SUM, RCP, PRB, TOP, PLACE, OVER, AT = (sc1[:, i, :] for i in range(8))

            with dve.Fori(0, NG) as g:
                n = g + (SC - 1) * NG
                weighted_hot(S, n, n)
                add_blocks(S, n, g)
                dve.drain()
                after(dve, S["drow_free"], g + 1)
                layernorm(g + NG, lambda u: acc[:, g * UN + u, :], lambda u: drow[:, u, D:2 * D], S["x2_ready"])
                dve.wait_ge(S["lg_ready"], g + 2)
                dve.tensor_reduce(MAXL, LG, AX.X, ALU.max)
                dve.drain()
                dve.tensor_tensor(smv(0), LG, wide(MAXL), ALU.subtract).then_inc(S["lmax_ready"], 1)
                dve.wait_ge(S["exp_ready"], g + 1)
                dve.tensor_reduce(SUM, smv(1), AX.X, ALU.add)
                dve.drain()
                dve.reciprocal(RCP, SUM)
                dve.drain()
                dve.tensor_tensor(smv(2), smv(1), wide(RCP), ALU.mult)
                dve.drain()
                dve.tensor_reduce(PRB, smv(2), AX.X, ALU.max)
                dve.drain()
                dve.tensor_tensor(smv(3), smv(2), wide(PRB), ALU.is_equal)
                dve.drain()
                dve.tensor_tensor(smv(3), smv(3), rev5, ALU.mult)
                dve.drain()
                dve.tensor_reduce(TOP, smv(3), AX.X, ALU.max)
                dve.drain()
                dve.tensor_tensor(smv(4), rev5, wide(TOP), ALU.is_equal)
                dve.drain()
                dve.tensor_tensor(smv(4), smv(4), wide(valid[:, bass.ds(g * UN, UN)]), ALU.mult)
                dve.drain()
                dve.tensor_copy(hot_e[:, :, :], smv(4)).then_inc(S["hote_ready"], 1)
                dve.wait_ge(S["pos_ready"], g + 1)
                dve.tensor_tensor(smv(5), POS, smv(4), ALU.mult)
                dve.tensor_reduce(hot_new[:, :], smv(4).rearrange("p u e -> p e u"), AX.X, ALU.add)
                dve.drain()
                dve.tensor_tensor(hot_sum[:, :], hot_sum[:, :], hot_new[:, :], ALU.add)
                dve.tensor_reduce(PLACE, smv(5), AX.X, ALU.add)
                dve.tensor_scalar(AT, TOP, -float(ROWS_E), float(N_EXP * ROWS_E - 1), ALU.mult, ALU.add)
                dve.drain()
                dve.tensor_tensor(AT, AT, PLACE, ALU.add)
                dve.tensor_scalar(OVER, PLACE, float(SLOTS), FAR, ALU.is_gt, ALU.mult)
                dve.tensor_scalar(SUM, PLACE, 0.5, FAR, ALU.is_lt, ALU.mult)
                dve.drain()
                dve.tensor_tensor(AT, AT, OVER, ALU.add)
                dve.tensor_copy(drow[:, :, 2 * D], PRB)
                dve.tensor_copy(drow[:, :, 2 * D + 1], token1[:, bass.ds(g * UN, UN)])
                dve.drain()
                dve.tensor_tensor(slot[:, :], AT, SUM, ALU.add)
                dve.drain()
                dve.wait_ge(S["x1_copied"], g * UN + UN)
                dve.sem_inc(S["slot_ready"], 1)

            with dve.Fori(0, N_EXP // 2) as q:
                for s in range(2):
                    dve.wait_ge(s_xs[s], 16 * q + 16)
                    dve.wait_ge(S["z_free"], 2 * q + (s + 1))
                    dve.tensor_scalar(tok_f[:, s, :], xs[:, s, :, 2 * D + 1], 0.5, FAR, ALU.is_lt, ALU.mult)
                    dve.drain()
                    dve.scalar_tensor_tensor(out=tok_f[:, s, :], in0=tok_f[:, s, :], scalar=-1.0,
                                             in1=xs[:, s, :, 2 * D + 1], op0=ALU.add, op1=ALU.add)
                    dve.drain()
                    dve.tensor_copy(tok[:, s, :], tok_f[:, s, :])
                    for t in range(NT):
                        rows = P if t < NT - 1 else SLOTS - (NT - 1) * P
                        z = z_sb[0:rows, t, :]
                        dve.wait_ge(S["y_ready"], 8 * q + (4 * s + t + 1))
                        dve.tensor_tensor(z, b(DOWN[t])[0:rows, 0:D], b2_all[0:rows, 2 * q + s, :], ALU.add
                                          ).then_inc(S["y_read"], 1)
                        dve.drain()
                        dve.tensor_scalar(z, z, xs[0:rows, s, t, 2 * D:2 * D + 1], None, ALU.mult)
                        dve.drain()
                        dve.tensor_tensor(odd[0:rows, 0, :], z, z, ALU.not_equal)
                        dve.tensor_scalar(odd[0:rows, 1, :], z, FLT_MAX, None, ALU.is_gt)
                        dve.tensor_scalar(odd[0:rows, 2, :], z, -FLT_MAX, None, ALU.is_lt)
                        for i in range(3):
                            dve.drain()
                            dve.copy_predicated(z, odd[0:rows, i, :], fills[0:rows, i, :])
                        dve.drain()
                        last = dve.tensor_tensor(z, z, xs[0:rows, s, t, 0:D], ALU.add)
                        last.then_inc(S["z_ready"], 1)
                    dve.drain()
                    dve.sem_inc(S["xs_free"], 1)

    return nc


_INS = ['x', 'src', 'dst', 'edge_weight', 'L0_gnn_weight_l', 'L0_gnn_bias_l', 'L0_gnn_weight_r', 'L0_gnn_bias_r',
        'L0_ffn_gate_w', 'L0_ffn_gate_b', 'L0_ffn_w1', 'L0_ffn_b1', 'L0_ffn_w2', 'L0_ffn_b2']


def kernel(**inputs):
    import numpy as _np
    import concourse.bacc as _bacc
    from concourse import mybir as _mybir
    from concourse.bass_utils import run_bass_kernel_spmd as _run

    nc = _bacc.Bacc("TRN2", target_bir_lowering=False, num_devices=1)
    arrays, args = {}, []
    for name in _INS:
        a = _np.ascontiguousarray(inputs[name])
        arrays[f"in_{name}_dram"] = a
        args.append(nc.dram_tensor(f"in_{name}_dram", a.shape, _mybir.dt.from_np(a.dtype), kind="ExternalInput").ap())
    h_rows = nc.dram_tensor("h_rows", (NB * P, D), _mybir.dt.float32, kind="Internal").ap()
    dispatch = nc.dram_tensor("dispatch", (N_EXP * ROWS_E, ROW), _mybir.dt.float32, kind="Internal").ap()
    out = nc.dram_tensor("out_0_dram", (N_NODES, D), _mybir.dt.float32, kind="ExternalOutput").ap()
    graph_moe(nc, *args, h_rows, dispatch, out)
    r = _run(nc, [arrays], core_ids=[0])
    return r.results[0]["out_0_dram"]
```

```python
import concourse.bass as bass
from concourse import mybir
from contextlib import ExitStack

P = 128
N_NODES, D, F_HID, N_EXP = 3125, 256, 1024, 8
N_EDGES = 53125
KD = D // P
KF = F_HID // P
NB = -(-N_NODES // P)
LAST = N_NODES - (NB - 1) * P
EP = 125
EC = N_EDGES // EP
SC = 5
CC = EC // SC
UN = 5
NG = NB // UN
PIECE = CC // NG
HALVES = ((0, (PIECE + 1) // 2), ((PIECE + 1) // 2, PIECE))
CAP = 512
NJ = CAP // P
REC = 6
ROUNDS = -(-EP * CC // CAP)
LW = NB * REC
SLOTS = 489
ROWS_E = 512
NT = ROWS_E // P
ROW = 2 * D + 2
EPS = 1e-5
FLT_MAX = 3.4028234663852886e38
FAR = 65536.0
assert EP * EC == N_EDGES and SC * CC == EC and NG * PIECE == CC and NG * UN == NB


def graph_moe(nc, x, src, dst, edge_weight, weight_l, bias_l, weight_r, bias_r,
              gate_w, gate_b, w1, b1, w2, b2, h_rows, dispatch, out):
    f32, bf16, f16 = mybir.dt.float32, mybir.dt.bfloat16, mybir.dt.float16
    i32, u32 = mybir.dt.int32, mybir.dt.uint32
    ALU = mybir.AluOpType
    ACT = mybir.ActivationFunctionType
    AX = mybir.AxisListType
    ctx = ExitStack()

    def sb(name, shape, dt):
        return ctx.enter_context(nc.sbuf_tensor(name, shape, dt))

    def pb(name, shape, dt=f32):
        return ctx.enter_context(nc.psum_tensor(name, shape, dt))

    def sem(name):
        return ctx.enter_context(nc.semaphore(name))

    with ctx:
        ident = sb("ident", [P, P], f32)
        before = sb("before", [EP, EP], bf16)
        upto = sb("upto", [P, P], bf16)
        ones = sb("ones", [P, P], bf16)
        ones_row = sb("ones_row", [1, P], f32)
        run = sb("run", [EP, NB * CC], bf16)
        iota_block = sb("iota_block", [P, NB], f32)
        iota_node = sb("iota_node", [P, P], f32)
        iota_i = sb("iota_i", [P, CAP], i32)
        iota_rank = sb("iota_rank", [P, CAP], f16)
        rev = sb("rev", [P, N_EXP], f32)
        token1 = sb("token1", [P, NB], f32)
        valid = sb("valid", [P, NB], f32)
        fills = sb("fills", [P, 3, D], f32)
        zero_row = sb("zero_row", [P, ROW], f32)
        zero_bf = sb("zero_bf", [P, LW], bf16)
        wlr = sb("wlr", [P, KD, 2 * D], f32)
        bias = sb("bias", [1, 2, D], f32)
        gw = sb("gw", [P, KD, N_EXP], f32)
        gb = sb("gb", [1, N_EXP], f32)
        b1_rows = sb("b1_rows", [N_EXP * KF, P], f32)
        b1_cols = sb("b1_cols", [P, N_EXP * KF], f32)
        b2_all = sb("b2_all", [P, N_EXP, D], f32)
        late = sb("late", [P, 2 * (KD * F_HID + KF * D)], f32)
        w1_sb = late[:, 0:2 * KD * F_HID].rearrange("p (s k f) -> p s k f", s=2, k=KD)
        w2_sb = late[:, 2 * KD * F_HID:].rearrange("p (s f d) -> p s f d", s=2, f=KF)
        at_rank = late[0:EP, 0:PIECE * CAP // 2].bitcast(bf16).rearrange("p (c r) -> p c r", c=PIECE)
        at_blk = late[0:EP, PIECE * CAP // 2:PIECE * (CAP + LW) // 2].bitcast(bf16).rearrange(
            "p (c l) -> p c l", c=PIECE)
        acc = sb("acc", [P, NB, D], f32)
        early = sb("early", [P, 2 * NB * D], f32)
        parts = {}

        def place(name, at, words, rows=P):
            parts[name] = (at, at + words)
            assert at + words <= 2 * NB * D
            return early[0:rows, at:at + words]

        xT = place("xT", 0, NB * D).rearrange("p (n d) -> p n d", d=D)
        h_sb = place("h", NB * D, NB * D).rearrange("p (n d) -> p n d", d=D)
        hot = place("hot", NB * D, UN * NJ * P).rearrange("p (n m) -> p n m", m=P)
        drow = place("drow", 0, 2 * UN * ROW).rearrange("p (s u w) -> p s u w", s=2, w=ROW)
        hid = place("hid", 0, 2 * KF * ROWS_E).rearrange("p (s f t) -> p s f t", s=2, f=KF)
        xnT = place("xnT", parts["hid"][1], 2 * KD * ROWS_E).rearrange("p (s k t) -> p s k t", s=2, k=KD)
        z_sb = place("z", parts["xnT"][1], NT * D).rearrange("p (t d) -> p t d", d=D)
        odd = place("odd", parts["z"][1], 3 * D).bitcast(i32).rearrange("p (i d) -> p i d", i=3)
        stats = sb("stats", [P, UN, 6], f32)
        moments = sb("moments", [P, NB, 2], f32)
        rstd = sb("rstd", [P, NB, 1], f32)
        moments2 = sb("moments2", [P, UN, 2], f32)
        rstd2 = sb("rstd2", [P, UN, 1], f32)
        xn = sb("xn", [P, UN, D], f32)
        xt = sb("xt", [P, UN, D], f32)
        xr = xn
        e_src = sb("e_src", [EP, EC], i32)
        e_dst = sb("e_dst", [EP, EC], i32)
        e_w = sb("e_w", [EP, EC], f32)
        landed = sb("landed", [P, max(UN * NJ * D, 2 * NT * ROW)], f32)
        fetched = landed[:, 0:UN * NJ * D].rearrange("p (n d) -> p n d", d=D)
        e_bits = landed[0:EP, 0:4 * EC].bitcast(i32).rearrange("p (i c) -> p i c", i=4)
        w_rest = landed[0:EP, 4 * EC:5 * EC]
        rank_top = sb("rank_top", [EP, 1], f32)
        rank_new = sb("rank_new", [1, 1], f32)
        rank_run = sb("rank_run", [1, 1], f32)
        rank_max = sb("rank_max", [1, 1], i32)
        blk = sb("blk", [EP, EC], f32)
        rec = sb("rec", [EP, EC, REC], bf16)
        in_blk = sb("in_blk", [EP, NB * CC], bf16)
        count = sb("count", [EP, NB * CC], f32)
        total = sb("total", [EP, NB], bf16)
        rank = sb("rank", [EP, EC], f32)
        t_dst = sb("t_dst", [P, (SC + 1) * NB * NJ], u32)
        tmp_dst = sb("tmp_dst", [P, NJ, NB], f32)
        t_src = sb("t_src", [P, (SC + 1) * NB * NJ], f32)
        t_w = sb("t_w", [P, (SC + 1) * NB * NJ], f32)
        idx = sb("idx", [P, UN, NJ], u32)
        sm = sb("sm", [P, 8, UN, N_EXP], f32)
        sc1 = sb("sc1", [P, 8, UN], f32)
        hot_e = sb("hot_e", [P, UN, N_EXP], bf16)
        hot_sum = sb("hot_sum", [P, N_EXP], bf16)
        hot_new = sb("hot_new", [P, N_EXP], f32)
        slot = sb("slot", [P, UN], u32)
        xs = landed[:, 0:2 * NT * ROW].rearrange("p (s t w) -> p s t w", s=2, t=NT)
        tok = sb("tok", [P, 2, NT], u32)
        tok_f = sb("tok_f", [P, 2, NT], f32)

        bank = [pb(f"bank{i}", [P, 512]) for i in range(4, 8)]
        ps_sort = pb("ps_sort", [P, 4, 512])

        def b(i):
            return ps_sort[:, i, :] if i < 4 else bank[i - 4][:, :]

        HL = (4, 5, 6, 4, 5)
        AG = (4, 5, 6, 4, 5)
        TP = (0, 1, 2, 3, 0)
        TP2 = (0, 1, 0, 1, 0)
        UP, DOWN = (2, 3, 4, 2, 3, 4, 2, 3), (5, 6, 7, 5)

        LG = [b(i)[:, 0:UN * N_EXP].rearrange("p (u e) -> p u e", e=N_EXP) for i in (2, 7)]
        POS = b(3)[:, 0:UN * N_EXP].rearrange("p (u e) -> p u e", e=N_EXP)

        def used(banks, u):
            n = len(banks)
            return next(v for v in range(n + u - 1, -1, -1) if banks[v % n] == banks[u]) + 1

        names = ("const passed consts2 edges_in w_in x_in x_ready bits_ready parts_ready wparts_ready total_ready base_ready "
                 "var_ready std_ready xn_ready tp_ready xt_ready hp_ready h_evac h_stored mom_ready calm block_ready row_ready xr_ready tail_ready "
                 "blk_ready rank_ready sort_used sort_done table_ready idx_ready hot_ready agg_done "
                 "acc_added zeroed x2_ready x1_copied tp2_ready xt2_ready lg_ready lmax_ready exp_ready "
                 "hote_ready pos_ready slot_ready drow_free dispatched x1_out "
                 "xs_free tpe_ready xte_ready hl_ready relu_done y_ready y_read z_ready z_free more_in b2_in b1_t b1_ready "
                 "top_ready top_t max_ready").split()
        S = {n: sem(n) for n in names}
        S["fetch"] = [sem(f"fetch{u}") for u in range(UN)]
        R = {n: sem("more_" + n) for n in ("rank_ready row_ready sort_used sort_done table_ready idx_ready hot_ready "
                                           "agg_done acc_added swept").split()}
        R["fetch"] = [sem(f"more_fetch{u}") for u in range(UN)]
        s_x = [sem(f"x_in{g}") for g in range(NG)]
        s_disp = [sem(f"disp{u}") for u in range(UN)]
        s_w = [sem(f"w_expert{i}") for i in range(2)]
        s_xs = [sem(f"xs_in{i}") for i in range(2)]
        s_out = [sem(f"out_tile{t}") for t in range(NT)]

        def after(eng, semaphore, value):
            eng.wait_ge(semaphore, value)
            eng.sem_inc(S["passed"], 1)

        def record_rows(eng, s, g, c0, c1):
            return eng.tensor_tensor(
                at_blk[:, c0:c1, :].rearrange("p c (b i) -> p c b i", i=REC),
                in_blk[:, :].rearrange("p (b c) -> p c b", c=CC)[:, bass.ds(g * PIECE + c0, c1 - c0), :, None]
                .broadcast_to([EP, c1 - c0, NB, REC]),
                rec[:, bass.ds(s * CC + g * PIECE + c0, c1 - c0), None, :].broadcast_to([EP, c1 - c0, NB, REC]),
                ALU.mult)

        def more_rounds(eng, free, body):
            eng.wait_ge(S["max_ready"], SC)
            largest = eng.value_load(rank_max[0:1, 0:1], min_val=0, max_val=EP * CC)
            with eng.If(largest > CAP):
                eng.wait_ge(S["calm"], 1)
                for name, n in free:
                    eng.sem_inc(R[name], n)
                with eng.Fori(1, ROUNDS) as r:
                    with eng.If(largest > r * CAP):
                        with eng.Fori(0, SC) as s:
                            k = (r - 1) * SC + s
                            body(s, k)
                            eng.wait_ge(R["swept"], k + 1)
                            eng.sem_inc(S["passed"], 1)

        block = ctx.enter_context(nc.Block())

        @block.sync
        def _(sp):
            e_view = "(p c) -> p c"
            sp.dma_start(e_src[:, :], src.rearrange(e_view, c=EC)).then_inc(S["edges_in"], 16)
            sp.dma_start(e_dst[:, :], dst.rearrange(e_view, c=EC)).then_inc(S["edges_in"], 16)
            sp.dma_start(e_w[:, :], edge_weight.rearrange(e_view, c=EC)).then_inc(S["edges_in"], 16)
            sp.wait_ge(S["consts2"], 1)
            for g in range(NG):
                n = UN if g < NG - 1 else UN - 1
                sp.dma_start(acc[:, g * UN:g * UN + n, :], x[g * UN * P:(g * UN + n) * P, :].rearrange(
                    "(n p) d -> p n d", p=P)).then_inc(s_x[g], 16)
            sp.dma_start(acc[0:LAST, NB - 1, :], x[(NB - 1) * P:N_NODES, :]).then_inc(s_x[NG - 1], 16)
            for k in range(KD):
                sp.dma_start(wlr[:, k, D:2 * D], weight_r[k * P:(k + 1) * P, :]).then_inc(S["more_in"], 16)
            sp.dma_start(bias[:, 0, :], bias_l[None, :]).then_inc(S["more_in"], 16)
            sp.dma_start(bias[:, 1, :], bias_r[None, :]).then_inc(S["more_in"], 16)
            sp.dma_start(gw[:, :, :], gate_w.rearrange("(k p) e -> p k e", p=P)).then_inc(S["more_in"], 16)
            sp.dma_start(gb[:, :], gate_b[None, :]).then_inc(S["more_in"], 16)
            sp.dma_start(b1_rows[:, :], b1.rearrange("e (f p) -> (e f) p", p=P)).then_inc(S["more_in"], 16)
            for g in range(NG):
                sp.wait_ge(s_x[g], 16 if g < NG - 1 else 32)
                sp.sem_inc(S["x_ready"], 1)
            with sp.Fori(0, NG) as g:
                sp.wait_ge(S["h_evac"], g * UN + 2 * UN)
                sp.dma_start(h_rows[bass.ds(g * (UN * P), UN * P), :].rearrange("(n p) d -> p n d", p=P),
                             h_sb[:, bass.ds(g * UN, UN), :]).then_inc(S["h_stored"], 16)
            sp.dma_start(b2_all[:, :, :].rearrange("p e d -> p (e d)"),
                         b2.rearrange("e d -> (e d)")[None, :].broadcast_to([P, N_EXP * D])
                         ).then_inc(S["b2_in"], 16)
            sp.wait_ge(S["zeroed"], 1)
            sp.dma_start(dispatch.rearrange("(n p) w -> p n w", p=P),
                         zero_row[:, None, :].broadcast_to([P, N_EXP * NT, ROW])).then_inc(S["dispatched"], 16)
            sp.wait_ge(S["table_ready"], SC)
            sp.wait_ge(S["max_ready"], SC)
            sp.wait_ge(S["tail_ready"], 1)
            for e in range(2):
                sp.dma_start(w1_sb[:, e, :, :], w1[e].rearrange("(k p) f -> p k f", p=P)).then_inc(s_w[e], 16)
                sp.dma_start(w2_sb[:, e, :, :], w2[e].rearrange("(f p) d -> p f d", p=P)).then_inc(s_w[e], 16)
            sp.wait_ge(S["acc_added"], SC * NB + UN)
            sp.dma_start(out[0:(NB - 1) * P, :].rearrange("(n p) d -> p n d", p=P), acc[:, 0:NB - 1, :]
                         ).then_inc(S["x1_out"], 16)
            sp.dma_start(out[(NB - 1) * P:N_NODES, :], acc[0:LAST, NB - 1, :]).then_inc(S["x1_out"], 16)

            def load_rows(e, s):
                sp.wait_ge(S["xs_free"], e + 1)
                sp.dma_start(xs[:, s, :, :], dispatch[bass.ds(e * ROWS_E, ROWS_E), :].rearrange(
                    "(t p) w -> p t w", p=P)).then_inc(s_xs[s], 16)

            sp.wait_ge(S["drow_free"], NG + 2)
            load_rows(0, 0)
            with sp.Fori(0, (N_EXP - 2) // 2) as q:
                for s in range(2):
                    load_rows(2 * q + (s + 1), 1 - s)
                    sp.wait_ge(S["y_ready"], 8 * q + 4 * (s + 1))
                    e2 = 2 * q + (s + 2)
                    sp.dma_start(w1_sb[:, s, :, :], w1[bass.ds(e2, 1)].rearrange("a (k p) f -> p (a k) f", p=P)
                                 ).then_inc(s_w[s], 16)
                    sp.dma_start(w2_sb[:, s, :, :], w2[bass.ds(e2, 1)].rearrange("a (f p) d -> p (a f) d", p=P)
                                 ).then_inc(s_w[s], 16)
            load_rows(N_EXP - 1, 1)

        @block.gpsimd
        def _(pool):
            pool.memset(acc[:, NB - 1, :], 0.0).then_inc(S["consts2"], 1)
            pool.memset(ident[:, :], 0.0)
            pool.memset(before[:, :], 1.0)
            pool.memset(upto[:, :], 1.0)
            pool.iota(iota_block[:, :], pattern=[[1, NB]], base=0, channel_multiplier=0,
                      allow_small_or_imprecise_dtypes=True)
            pool.iota(iota_node[:, :], pattern=[[1, P]], base=0, channel_multiplier=0,
                      allow_small_or_imprecise_dtypes=True)
            pool.iota(iota_i[:, :], pattern=[[1, CAP]], base=1, channel_multiplier=0)
            pool.iota(rev[:, :], pattern=[[-1, N_EXP]], base=N_EXP, channel_multiplier=0,
                      allow_small_or_imprecise_dtypes=True)
            pool.iota(token1[:, :], pattern=[[P, NB]], base=1, channel_multiplier=1,
                      allow_small_or_imprecise_dtypes=True)
            pool.memset(ones[:, :], 1.0)
            pool.memset(ones_row[:, :], 1.0)
            pool.memset(run[:, :], 1.0)
            pool.memset(fills[:, 0, :], 0.0)
            pool.memset(fills[:, 1, :], 1e4)
            pool.memset(fills[:, 2, :], -1e4)
            pool.memset(hot_sum[:, :], 0.0)
            pool.drain()
            pool.memset(run[:, :].rearrange("p (b c) -> p b c", c=CC)[:, :, 0:1], 0.0)
            pool.affine_select(out=ident[:, :], in_=ident[:, :], compare_op=ALU.not_equal, fill=1.0,
                               base=0, pattern=[[-1, P]], channel_multiplier=1)
            pool.affine_select(out=before[:, :], in_=before[:, :], compare_op=ALU.is_gt, fill=0.0,
                               base=0, pattern=[[1, EP]], channel_multiplier=-1)
            pool.affine_select(out=upto[:, :], in_=upto[:, :], compare_op=ALU.is_ge, fill=0.0,
                               base=0, pattern=[[1, P]], channel_multiplier=-1)
            pool.drain()
            pool.memset(zero_row[:, :], 0.0).then_inc(S["zeroed"], 1)
            pool.drain()
            pool.sem_inc(S["const"], 1)
            pool.wait_ge(S["edges_in"], 48)
            pool.tensor_copy(rec[:, :, 3], e_w[:, :])
            pool.drain()
            pool.tensor_tensor(w_rest, e_w[:, :], rec[:, :, 3], ALU.subtract)
            pool.drain()
            pool.tensor_copy(rec[:, :, 4], w_rest)
            pool.drain()
            pool.tensor_tensor(rec[:, :, 5], w_rest, rec[:, :, 4], ALU.subtract
                               ).then_inc(S["wparts_ready"], 1)
            def rows(g):
                for c0, c1 in HALVES:
                    after(pool, S["sort_used"], 2 * g + (1 if c0 == 0 else 2))
                    record_rows(pool, 0, g, c0, c1).then_inc(S["row_ready"], 1)

            pool.drain()
            pool.wait_ge(S["block_ready"], 1)
            pool.wait_ge(S["parts_ready"], 1)
            with pool.Fori(0, NG) as g:
                rows(g)

            def gathers(Q, n, us=range(UN)):
                for u in us:
                    after(pool, Q["idx_ready"], n * UN + (u + 1))
                    for j in range(NJ):
                        pool.indirect_dma_start(
                            fetched[:, u * NJ + j, :], None, h_rows,
                            bass.IndirectOffsetOnAxis(ap=idx[:, u, j:j + 1], axis=0)).then_inc(Q["fetch"][u], 16)

            def scatters(g, d):
                for u in range(UN):
                    after(pool, S["slot_ready"], g + 1)
                    pool.indirect_dma_start(
                        dispatch, bass.IndirectOffsetOnAxis(ap=slot[:, u:u + 1], axis=0), drow[:, d, u, :], None,
                        bounds_check=N_EXP * ROWS_E - 1, oob_is_err=False).then_inc(s_disp[u], 16)

            def scattered(g):
                for u in range(UN):
                    after(pool, s_disp[u], (g + 1) * 16)
                pool.sem_inc(S["drow_free"], 1)

            pool.wait_ge(S["h_stored"], NG * 16)
            with pool.Fori(0, (SC - 1) * NG) as n:
                gathers(S, n)

            def more(s, k):
                with pool.Fori(0, NG) as g:
                    gathers(R, k * NG + g)

            more_rounds(pool, (), more)
            gathers(S, (SC - 1) * NG)
            pool.wait_ge(S["dispatched"], 16)

            def route(g, d, later=True):
                gathers(S, g + (SC - 1) * NG, range(1, UN))
                scatters(g - 1, 1 - d)
                if later:
                    gathers(S, g + ((SC - 1) * NG + 1), range(0, 1))
                scattered(g - 1)

            gathers(S, (SC - 1) * NG + 1, range(0, 1))
            with pool.Fori(0, (NG - 3) // 2) as q:
                for i in range(2):
                    route(2 * q + (1 + i), 1 - i)
            route(NG - 2, 1)
            route(NG - 1, 0, later=False)
            scatters(NG - 1, 0)
            scattered(NG - 1)
            pool.wait_ge(S["x1_out"], 32)
            with pool.Fori(0, N_EXP // 2) as q:
                for s in range(2):
                    for t in range(NT):
                        rows = P if t < NT - 1 else SLOTS - (NT - 1) * P
                        after(pool, S["z_ready"], 8 * q + (4 * s + t + 1))
                        pool.indirect_dma_start(
                            out, bass.IndirectOffsetOnAxis(ap=tok[0:rows, s, t:t + 1], axis=0),
                            z_sb[0:rows, t, :], None,
                            bounds_check=N_NODES - 1, oob_is_err=False).then_inc(s_out[t], 16)
                    for t in range(NT):
                        after(pool, s_out[t], 32 * q + 16 * (s + 1))
                    pool.sem_inc(S["z_free"], 1)

        @block.scalar
        def _(act):
            for k in range(KD):
                act.dma_start(wlr[:, k, 0:D], weight_l[k * P:(k + 1) * P, :]).then_inc(S["w_in"], 16)
            act.sem_inc(S["xt_ready"], UN)
            act.sem_inc(S["h_evac"], UN)

            def root(i, dev):
                act.wait_ge(S["var_ready"], i + 1)
                act.activation(dev, dev, ACT.Sqrt).then_inc(S["std_ready"], 1)

            for g in range(2):
                root(g, rstd[:, g * UN:(g + 1) * UN, :])
            act.wait_ge(S["bits_ready"], 1)
            act.activation(blk[:, :], e_bits[:, 0, :], ACT.Copy)
            for i in range(3):
                last = act.activation(rec[:, :, i], e_bits[:, i + 1, :], ACT.Copy)
            act.drain()
            act.sem_inc(S["parts_ready"], 1)

            for g in range(NG):
                if 2 <= g + 1 < NG:
                    root(g + 1, rstd[:, (g + 1) * UN:(g + 2) * UN, :])
                for t in range(g * UN, (g + 1) * UN):
                    act.wait_ge(S["tp_ready"], UN + t + 1)
                    act.activation(xT[:, t, :], b(TP[t % UN])[:, 0:D], ACT.Copy).then_inc(S["xt_ready"], 1)
                for t in range(g * UN, (g + 1) * UN):
                    act.wait_ge(S["hp_ready"], UN + t + 1)
                    act.activation(h_sb[:, t, :], b(HL[t % UN])[:, 0:D], ACT.Copy).then_inc(S["h_evac"], 1)

            act.wait_ge(S["b1_t"], 1)
            act.activation(b1_cols[:, :], b(7)[:, 0:N_EXP * KF], ACT.Copy).then_inc(S["b1_ready"], 1)

            def copy_idx(Q, at, n, u):
                act.wait_ge(Q["agg_done"], n * UN + (u + 1))
                act.activation(idx[:, u, :], t_dst[:, bass.ds(at * (UN * NJ) + u * NJ, NJ)], ACT.Copy
                               ).then_inc(Q["idx_ready"], 1)

            act.wait_ge(S["table_ready"], 1)
            with act.Fori(0, NG) as g:
                for u in range(UN):
                    copy_idx(S, g, g, u)
                    act.activation(xr[:, u, :], xT[:, g * UN + u, :], ACT.Copy).then_inc(S["xr_ready"], 1)
            with act.Fori(1, SC - 1) as s:
                act.wait_ge(S["table_ready"], s + 1)
                with act.Fori(0, NG) as g:
                    for u in range(UN):
                        copy_idx(S, s * NG + g, s * NG + g, u)

            def more(s, k):
                act.wait_ge(R["table_ready"], k + 1)
                with act.Fori(0, NG) as g:
                    for u in range(UN):
                        copy_idx(R, g + SC * NG, k * NG + g, u)

            more_rounds(act, (), more)
            act.wait_ge(S["table_ready"], SC)
            for u in range(UN):
                copy_idx(S, (SC - 1) * NG, (SC - 1) * NG, u)

            def exponent(g):
                act.wait_ge(S["lmax_ready"], g + 1)
                act.activation(sm[:, 1, :, :], sm[:, 0, :, :], ACT.Exp).then_inc(S["exp_ready"], 1)

            def turned(g, u):
                act.wait_ge(S["tp2_ready"], g * UN + (u + 1))
                act.wait_ge(S["lg_ready"], g * UN + (u + 1))
                act.activation(xt[:, u, :], b(TP2[u])[:, 0:D], ACT.Copy).then_inc(S["xt2_ready"], 1)

            def route(g, d, later=True):
                act.wait_ge(S["drow_free"], g + 1)
                for u in range(UN):
                    if later:
                        copy_idx(S, g + ((SC - 1) * NG + 1), g + ((SC - 1) * NG + 1), u)
                    act.wait_ge(S["acc_added"], g * UN + ((SC - 1) * NB + UN + u + 1))
                    act.activation(drow[:, d, u, 0:D], acc[:, g * UN + u, :], ACT.Copy).then_inc(S["x1_copied"], 1)
                    if u > 0:
                        turned(g, u - 1)
                    root(g * UN + (NG + u), rstd2[:, u, :])
                turned(g, UN - 1)
                exponent(g)

            route(0, 0)
            with act.Fori(0, (NG - 3) // 2) as q:
                for i in range(2):
                    route(2 * q + (1 + i), 1 - i)
            route(NG - 2, 1)
            route(NG - 1, 0, later=False)

            act.wait_ge(S["b1_ready"], 1)
            with act.Fori(0, N_EXP // 2) as q:
                for s in range(2):
                    for k in range(KD):
                        act.wait_ge(S["tpe_ready"], 4 * q + (2 * s + k + 1))
                        act.activation(xnT[:, s, k, :], b(k), ACT.Copy).then_inc(S["xte_ready"], 1)
                    for f in range(KF):
                        act.wait_ge(S["hl_ready"], 16 * q + (8 * s + f + 1))
                        act.activation(hid[:, s, f, 0:SLOTS], b(UP[f])[:, 0:SLOTS], ACT.Relu,
                                       bias=b1_cols[:, bass.ds(16 * q + (8 * s + f), 1)]
                                       ).then_inc(S["relu_done"], 1)

        @block.tensor
        def _(pe):
            pe.sem_inc(S["agg_done"], UN)
            pe.sem_inc(S["tp_ready"], UN)

            pe.sem_inc(S["hp_ready"], UN)
            pe.sem_inc(S["sort_used"], 2)
            pe.sem_inc(S["lg_ready"], UN)
            pe.wait_ge(S["const"], 1)
            pe.wait_ge(S["w_in"], 16 * KD)

            def project(g):
                for u in range(UN):
                    t = g * UN + u
                    pe.wait_ge(S["xn_ready"], t + 1)
                    pe.wait_ge(S["xt_ready"], g * UN + used(TP, u))
                    for k in range(KD):
                        last = pe.transpose(b(TP[u])[:, k * P:(k + 1) * P], xn[:, u, k * P:(k + 1) * P], ident[:, :])
                    last.then_inc(S["tp_ready"], 1)
                for u in range(UN):
                    t = g * UN + u
                    pe.wait_ge(S["xt_ready"], UN + t + 1)
                    pe.wait_ge(S["h_evac"], g * UN + used(HL, u))
                    for k in range(KD):
                        last = pe.matmul(b(HL[u])[:, 0:D], lhsT=xT[:, t, k * P:(k + 1) * P],
                                         rhs=wlr[:, k, 0:D], start=(k == 0), stop=(k == KD - 1))
                    last.then_inc(S["hp_ready"], 1)

            def base(s):
                pe.wait_ge(S["total_ready"], s + 1)
                pe.matmul(b(7)[0:EP, 0:NB], lhsT=before[:, :], rhs=total[:, :], start=True, stop=True
                          ).then_inc(S["base_ready"], 1)

            def open_sort():
                for j in range(NJ):
                    pe.matmul(ps_sort[:, j, 0:LW], lhsT=zero_bf[0:EP, 0:P], rhs=zero_bf[0:EP, 0:LW],
                              start=True, stop=False)

            def close_sort(Q):
                for j in range(NJ):
                    last = pe.matmul(ps_sort[:, j, 0:LW], lhsT=zero_bf[0:EP, 0:P], rhs=zero_bf[0:EP, 0:LW],
                                     start=False, stop=True)
                last.then_inc(Q["sort_done"], 1)

            def sort_piece(Q, m):
                for i, (c0, c1) in enumerate(HALVES):
                    pe.wait_ge(Q["row_ready"], 2 * m + (i + 1))
                    for c in range(c0, c1):
                        pe.wait_ge(Q["rank_ready"], m * PIECE + (c + 1))
                        for j in range(NJ):
                            last = pe.matmul(ps_sort[:, j, 0:LW], lhsT=at_rank[:, c, j * P:(j + 1) * P],
                                             rhs=at_blk[:, c, :], start=False, stop=False)
                    last.then_inc(Q["sort_used"], 1)

            def aggregate(Q, n, us=range(UN), own=False):
                for u in us:
                    pe.wait_ge(Q["acc_added"], n * UN + used(AG, u))
                    if own:
                        pe.wait_ge(S["xr_ready"], n * UN + (u + 1))
                        for k in range(KD):
                            pe.matmul(b(AG[u])[:, 0:D], lhsT=xr[:, u, k * P:(k + 1) * P],
                                      rhs=wlr[:, k, D:2 * D], start=(k == 0), stop=False)
                        for i in range(2):
                            pe.matmul(b(AG[u])[:, 0:D], lhsT=ones_row[:, :], rhs=bias[:, i, :],
                                      start=False, stop=False)
                    pe.wait_ge(Q["fetch"][u], n * (16 * NJ) + 16 * NJ)
                    pe.wait_ge(Q["hot_ready"], n * (UN * NJ) + (u + 1) * NJ)
                    for j in range(NJ):
                        last = pe.matmul(b(AG[u])[:, 0:D], lhsT=hot[:, u * NJ + j, :],
                                         rhs=fetched[:, u * NJ + j, :],
                                         start=(j == 0 and not own), stop=(j == NJ - 1))
                    last.then_inc(Q["agg_done"], 1)

            project(0)
            project(1)
            base(0)
            for g in range(2, NG):
                project(g)
            open_sort()
            for g in range(NG):
                sort_piece(S, g)
            close_sort(S)

            def top(s):
                pe.wait_ge(S["top_ready"], s + 1)
                pe.transpose(b(7)[0:1, 0:EP], rank_top[:, :], ident[0:EP, 0:EP]).then_inc(S["top_t"], 1)

            top(0)
            pe.wait_ge(S["max_ready"], 1)
            pe.wait_ge(S["more_in"], 16 * (KD + 5))
            pe.transpose(b(7)[:, 0:N_EXP * KF], b1_rows[:, :], ident[0:N_EXP * KF, 0:N_EXP * KF]
                         ).then_inc(S["b1_t"], 1)
            pe.wait_ge(S["b1_ready"], 1)

            def sum_and_sort(s, own):
                aggregate(S, s * NG, range(0, 2), own)
                base(s + 1)
                aggregate(S, s * NG, range(2, UN), own)
                top(s + 1)
                pe.wait_ge(S["table_ready"], s + 1)
                open_sort()
                sort_piece(S, (s + 1) * NG)
                with pe.Fori(1, NG - 1) as g:
                    aggregate(S, g + s * NG, own=own)
                    sort_piece(S, g + (s + 1) * NG)
                sort_piece(S, (s + 1) * NG + (NG - 1))
                close_sort(S)
                aggregate(S, s * NG + (NG - 1), own=own)

            sum_and_sort(0, True)
            with pe.Fori(1, SC - 1) as s:
                sum_and_sort(s, False)

            def more(s, k):
                open_sort()
                with pe.Fori(0, NG) as g:
                    sort_piece(R, k * NG + g)
                close_sort(R)
                with pe.Fori(0, NG) as g:
                    aggregate(R, k * NG + g)

            more_rounds(pe, (("agg_done", UN), ("sort_used", 2)), more)

            def turn(g, d, u):
                pe.wait_ge(S["x2_ready"], g * UN + (u + 1))
                pe.wait_ge(S["xt2_ready"], g * UN + used(TP2, u))
                for k in range(KD):
                    last = pe.transpose(b(TP2[u])[:, k * P:(k + 1) * P],
                                        drow[:, d, u, D + k * P:D + (k + 1) * P], ident[:, :])
                last.then_inc(S["tp2_ready"], 1)

            def logits(g, d, u):
                pe.wait_ge(S["xt2_ready"], g * UN + (UN + u + 1))
                for k in range(KD):
                    pe.matmul(LG[d][:, u, :], lhsT=xt[:, u, k * P:(k + 1) * P], rhs=gw[:, k, :],
                              start=(k == 0), stop=False)
                pe.matmul(LG[d][:, u, :], lhsT=ones_row[:, :], rhs=gb[:, :], start=False, stop=True
                          ).then_inc(S["lg_ready"], 1)

            def position(g):
                pe.wait_ge(S["hote_ready"], g + 1)
                for u in range(UN):
                    pe.matmul(POS[:, u, :], lhsT=ones[:, :], rhs=hot_sum[:, :], start=True, stop=False)
                    for v in range(u):
                        pe.matmul(POS[:, u, :], lhsT=ones[:, :], rhs=hot_e[:, v, :], start=False, stop=False)
                    last = pe.matmul(POS[:, u, :], lhsT=upto[:, :], rhs=hot_e[:, u, :], start=False, stop=True)
                last.then_inc(S["pos_ready"], 1)

            def route(g, d, before=True):
                n = g + (SC - 1) * NG
                for u in range(UN):
                    aggregate(S, n, (u,))
                    if u == 0 and before:
                        position(g - 1)
                    if u > 0:
                        turn(g, d, u - 1)
                    if u > 1:
                        logits(g, d, u - 2)
                logits(g, d, UN - 2)
                turn(g, d, UN - 1)
                logits(g, d, UN - 1)

            route(0, 0, before=False)
            with pe.Fori(0, (NG - 1) // 2) as q:
                for i in range(2):
                    route(2 * q + (1 + i), 1 - i)
            position(NG - 1)

            def turn_rows(e, s):
                pe.wait_ge(s_xs[s], 8 * (e - s) + 16)
                pe.wait_ge(S["xte_ready"], 2 * e + 2)
                for k in range(KD):
                    for t in range(NT):
                        last = pe.transpose(b(k)[:, t * P:(t + 1) * P], xs[:, s, t, D + k * P:D + (k + 1) * P],
                                            ident[:, :])
                    last.then_inc(S["tpe_ready"], 1)

            def up(e, s):
                pe.wait_ge(s_w[s], 16 * (e - s) + 32)
                pe.wait_ge(S["xte_ready"], 2 * e + 4)
                for f in range(KF):
                    pe.wait_ge(S["relu_done"], 8 * e + used(UP, f))
                    for k in range(KD):
                        last = pe.matmul(b(UP[f])[:, 0:SLOTS], lhsT=w1_sb[:, s, k, f * P:(f + 1) * P],
                                         rhs=xnT[:, s, k, 0:SLOTS], start=(k == 0), stop=(k == KD - 1))
                    last.then_inc(S["hl_ready"], 1)

            def down(e, s):
                pe.wait_ge(S["relu_done"], 8 * e + 2 * KF)
                for t in range(NT):
                    rows = P if t < NT - 1 else SLOTS - (NT - 1) * P
                    pe.wait_ge(S["y_read"], 4 * e + used(DOWN, t))
                    for f in range(KF):
                        last = pe.matmul(b(DOWN[t])[0:rows, 0:D], lhsT=hid[:, s, f, t * P:t * P + rows],
                                         rhs=w2_sb[:, s, f, :], start=(f == 0), stop=(f == KF - 1))
                    last.then_inc(S["y_ready"], 1)

            turn_rows(0, 0)
            up(0, 0)
            with pe.Fori(0, (N_EXP - 2) // 2) as q:
                turn_rows(2 * q + 1, 1)
                down(2 * q, 0)
                up(2 * q + 1, 1)
                turn_rows(2 * q + 2, 0)
                down(2 * q + 1, 1)
                up(2 * q + 2, 0)
            turn_rows(N_EXP - 1, 1)
            down(N_EXP - 2, 0)
            up(N_EXP - 1, 1)
            down(N_EXP - 1, 1)

        @block.vector
        def _(dve):
            dve.sem_inc(S["acc_added"], UN)
            dve.sem_inc(S["xt2_ready"], UN)
            dve.sem_inc(S["xte_ready"], 2)
            dve.sem_inc(S["relu_done"], KF)
            dve.sem_inc(S["y_read"], NT)
            dve.sem_inc(S["xs_free"], 2)
            dve.sem_inc(S["z_free"], 1)
            dve.sem_inc(S["drow_free"], 2)
            dve.memset(zero_bf[:, :], 0.0)
            dve.memset(rank_run[:, :], 0.0)
            dve.wait_ge(S["edges_in"], 48)
            for i, (data, op, by) in enumerate(((e_src, ALU.logical_shift_right, 7), (e_src, ALU.bitwise_and, 127),
                                                (e_dst, ALU.logical_shift_right, 4), (e_dst, ALU.bitwise_and, 15))):
                last = dve.tensor_scalar(e_bits[:, i, :], data[:, :], by, None, op)
            last.then_inc(S["bits_ready"], 1)
            dve.wait_ge(S["const"], 1)
            dve.tensor_copy(iota_rank[:, :], iota_i[:, :])
            dve.tensor_scalar(valid[:, :], token1[:, :], float(N_NODES), None, ALU.is_le)

            blkT = in_blk[:, :].rearrange("p (b c) -> p b c", c=CC)
            countT = count[:, :].rearrange("p (b c) -> p b c", c=CC)

            def block_hot(s):
                dve.tensor_tensor(blkT, blk[:, None, bass.ds(s * CC, CC)].broadcast_to([EP, NB, CC]),
                                  iota_block[0:EP, :, None].broadcast_to([EP, NB, CC]), ALU.is_equal)
                dve.drain()

            def running_count(s):
                dve.tensor_tensor_scan(count[:, :], run[:, :], in_blk[:, :], 0.0, ALU.mult, ALU.add)
                dve.drain()
                dve.tensor_copy(total[:, :], countT[:, :, CC - 1]).then_inc(S["total_ready"], 1)

            def place_count(s):
                dve.wait_ge(S["base_ready"], s + 1)
                dve.tensor_tensor(countT, countT, b(7)[0:EP, 0:NB, None].broadcast_to([EP, NB, CC]), ALU.add)
                dve.drain()
                dve.tensor_tensor(count[:, :], count[:, :], in_blk[:, :], ALU.mult)
                dve.drain()
                dve.tensor_reduce(rank[:, bass.ds(s * CC, CC)], count[:, :].rearrange("p (b c) -> p c b", c=CC),
                                  AX.X, ALU.add)
                dve.drain()

            def ranks(s):
                block_hot(s)
                dve.sem_inc(S["block_ready"], 1)
                running_count(s)
                place_count(s)

            def build_piece(Q, s, g, m, rows=True):
                for c0, c1 in HALVES:
                    dve.wait_ge(Q["sort_used"], 2 * m + (1 if c0 == 0 else 2))
                    if rows:
                        record_rows(dve, s, g, c0, c1).then_inc(Q["row_ready"], 1)
                    for c in range(c0, c1):
                        dve.tensor_scalar(at_rank[:, c, :], iota_rank[0:EP, :],
                                          rank[:, bass.ds(s * CC + g * PIECE + c, 1)], None,
                                          ALU.is_equal).then_inc(Q["rank_ready"], 1)

            def take_table(Q, at, k):
                dve.wait_ge(Q["sort_done"], k + 1)

                def part(i):
                    return ps_sort[:, 0:NJ, 0:LW].rearrange("p j (b i) -> p j b i", i=REC)[:, :, :, i]

                def table(t):
                    return t[:, bass.ds(at * (NB * NJ), NB * NJ)].rearrange("p (b j) -> p j b", j=NJ)

                dve.tensor_copy(table(t_src), part(0))
                dve.tensor_copy(table(t_w), part(3))
                dve.tensor_scalar(tmp_dst[:, :, :], part(1), 16.0, None, ALU.mult)
                dve.drain()
                dve.tensor_tensor(table(t_w), table(t_w), part(4), ALU.add)
                dve.tensor_tensor(table(t_dst), tmp_dst[:, :, :], part(2), ALU.add)
                dve.drain()
                dve.tensor_tensor(table(t_w), table(t_w), part(5), ALU.add)
                dve.drain()
                dve.sem_inc(Q["table_ready"], 1)

            def weighted_hot(Q, at_n, n, us=range(UN)):
                for u in us:
                    dve.wait_ge(Q["agg_done"], n * UN + (u + 1))
                    for j in range(NJ):
                        at = at_n * (UN * NJ) + (u * NJ + j)
                        dve.tensor_scalar(hot[:, u * NJ + j, :], iota_node[:, :], t_src[:, bass.ds(at, 1)],
                                          t_w[:, bass.ds(at, 1)], ALU.is_equal, ALU.mult
                                          ).then_inc(Q["hot_ready"], 1)

            def add_and_next(n, g, us=range(UN), later=True):
                for u in us:
                    add_blocks(S, n, g, (u,))
                    if later:
                        weighted_hot(S, n + 1, n + 1, (u,))

            def add_blocks(Q, n, g, us=range(UN)):
                for u in us:
                    dve.wait_ge(Q["agg_done"], n * UN + (UN + u + 1))
                    dve.tensor_tensor(acc[:, g * UN + u, :], acc[:, g * UN + u, :], b(AG[u])[:, 0:D], ALU.add
                                      ).then_inc(Q["acc_added"], 1)

            def moment(rows, mom, dev):
                for i, row in enumerate(rows):
                    dve.bn_stats(stats[:, i, :], row)
                dve.drain()
                for i in range(len(rows)):
                    dve.bn_aggr(mom[:, i, :], stats[:, i, :])
                dve.drain()
                dve.tensor_scalar(dev, mom[:, :, 1:2], EPS, None, ALU.add).then_inc(S["var_ready"], 1)

            def invert(i, dev):
                dve.wait_ge(S["std_ready"], i + 1)
                dve.reciprocal(dev, dev)
                dve.drain()

            def spread(g):
                own = slice(g * UN, g * UN + UN)
                dve.wait_ge(S["x_ready"], g + 1)
                moment([acc[:, t, :] for t in range(g * UN, g * UN + UN)], moments[:, own, :], rstd[:, own, :])

            def normalize(g):
                invert(g, rstd[:, g * UN:g * UN + UN, :])
                for u in range(UN):
                    t = g * UN + u
                    dve.wait_ge(S["tp_ready"], t + 1)
                    dve.tensor_scalar(xn[:, u, :], acc[:, t, :], moments[:, t, 0:1], rstd[:, t, :],
                                      ALU.subtract, ALU.mult).then_inc(S["xn_ready"], 1)

            def top(s):
                dve.tensor_reduce(rank_top[:, :], rank[:, bass.ds(s * CC, CC)], AX.X, ALU.max
                                  ).then_inc(S["top_ready"], 1)

            def keep_top(s):
                dve.wait_ge(S["top_t"], s + 1)
                dve.tensor_reduce(rank_new[:, :], b(7)[0:1, 0:EP], AX.X, ALU.max)
                dve.drain()
                dve.tensor_tensor(rank_run[:, :], rank_run[:, :], rank_new[:, :], ALU.max)
                dve.drain()
                dve.tensor_copy(rank_max[:, :], rank_run[:, :]).then_inc(S["max_ready"], 1)

            spread(0)
            spread(1)
            normalize(0)
            spread(2)
            normalize(1)
            dve.wait_ge(S["parts_ready"], 1)
            block_hot(0)
            dve.sem_inc(S["block_ready"], 1)
            running_count(0)
            normalize(2)
            spread(3)
            place_count(0)
            top(0)
            normalize(3)
            spread(4)
            normalize(4)
            for g in range(NG):
                build_piece(S, 0, g, g, rows=False)
            take_table(S, 0, 0)
            keep_top(0)
            dve.wait_ge(S["h_stored"], NG * 16)
            weighted_hot(S, 0, 0)
            dve.wait_ge(S["wparts_ready"], 1)
            with dve.Fori(0, SC - 1) as s:
                n0 = s * NG
                block_hot(s + 1)
                running_count(s + 1)
                add_and_next(n0, 0, range(0, 2))
                place_count(s + 1)
                top(s + 1)
                add_and_next(n0, 0, range(2, UN))
                build_piece(S, s + 1, 0, n0 + NG)
                keep_top(s + 1)
                with dve.Fori(1, NG - 1) as g:
                    build_piece(S, s + 1, g, n0 + NG + g)
                    add_and_next(n0 + g, g)
                build_piece(S, s + 1, NG - 1, n0 + (2 * NG - 1))
                take_table(S, s + 1, s + 1)
                add_and_next(n0 + (NG - 1), NG - 1)
            dve.drain()
            dve.sem_inc(S["calm"], 1)

            def more(s, k):
                with dve.If(s == 0):
                    dve.tensor_scalar(rank[:, :], rank[:, :], float(-CAP), None, ALU.add)
                    dve.drain()
                block_hot(s)
                with dve.Fori(0, NG) as g:
                    build_piece(R, s, g, k * NG + g)
                take_table(R, SC, k)
                with dve.Fori(0, NG) as g:
                    weighted_hot(R, g + SC * NG, k * NG + g)
                    add_blocks(R, k * NG + g, g)
                for u in range(UN):
                    for j in range(NJ):
                        at = (SC - 1) * NG * UN * NJ + u * NJ + j
                        dve.tensor_scalar(hot[:, u * NJ + j, :], iota_node[:, :], t_src[:, at:at + 1],
                                          t_w[:, at:at + 1], ALU.is_equal, ALU.mult)
                dve.drain()
                dve.sem_inc(R["swept"], 1)

            more_rounds(dve, (("acc_added", UN),), more)
            dve.sem_inc(S["tail_ready"], 1)

            def smv(i):
                return sm[:, i, :, :]

            def wide(ap):
                return ap[:, :, None].broadcast_to([P, UN, N_EXP])

            rev5 = rev[:, None, :].broadcast_to([P, UN, N_EXP])
            MAXL, SUM, RCP, PRB, TOP, PLACE, OVER, AT = (sc1[:, i, :] for i in range(8))

            def block(g, d, u, later):
                n = g + (SC - 1) * NG
                add_and_next(n, g, (u,), later)
                dve.drain()
                moment([acc[:, g * UN + u, :]], moments2[:, u:u + 1, :], rstd2[:, u:u + 1, :])
                invert(g * UN + (NG + u), rstd2[:, u, :])
                dve.tensor_scalar(drow[:, d, u, D:2 * D], acc[:, g * UN + u, :], moments2[:, u, 0:1],
                                  rstd2[:, u, :], ALU.subtract, ALU.mult).then_inc(S["x2_ready"], 1)

            def choose(g, d):
                dve.wait_ge(S["lg_ready"], g * UN + 2 * UN)
                dve.tensor_reduce(MAXL, LG[d], AX.X, ALU.max)
                dve.drain()
                dve.tensor_tensor(smv(0), LG[d], wide(MAXL), ALU.subtract).then_inc(S["lmax_ready"], 1)
                dve.wait_ge(S["exp_ready"], g + 1)
                dve.tensor_reduce(SUM, smv(1), AX.X, ALU.add)
                dve.drain()
                dve.reciprocal(RCP, SUM)
                dve.drain()
                dve.tensor_tensor(smv(2), smv(1), wide(RCP), ALU.mult)
                dve.drain()
                dve.tensor_reduce(PRB, smv(2), AX.X, ALU.max)
                dve.drain()
                dve.tensor_tensor(smv(3), smv(2), wide(PRB), ALU.is_equal)
                dve.drain()
                dve.tensor_tensor(smv(3), smv(3), rev5, ALU.mult)
                dve.drain()
                dve.tensor_reduce(TOP, smv(3), AX.X, ALU.max)
                dve.drain()
                dve.tensor_tensor(smv(4), rev5, wide(TOP), ALU.is_equal)
                dve.drain()
                dve.tensor_tensor(smv(4), smv(4), wide(valid[:, bass.ds(g * UN, UN)]), ALU.mult)
                dve.drain()
                dve.tensor_copy(hot_e[:, :, :], smv(4)).then_inc(S["hote_ready"], 1)

            def queue(g, d):
                dve.wait_ge(S["pos_ready"], g + 1)
                dve.tensor_tensor(smv(5), POS, smv(4), ALU.mult)
                dve.tensor_reduce(hot_new[:, :], smv(4).rearrange("p u e -> p e u"), AX.X, ALU.add)
                dve.drain()
                dve.tensor_tensor(hot_sum[:, :], hot_sum[:, :], hot_new[:, :], ALU.add)
                dve.tensor_reduce(PLACE, smv(5), AX.X, ALU.add)
                dve.tensor_scalar(AT, TOP, -float(ROWS_E), float(N_EXP * ROWS_E - 1), ALU.mult, ALU.add)
                dve.drain()
                dve.tensor_tensor(AT, AT, PLACE, ALU.add)
                dve.tensor_scalar(OVER, PLACE, float(SLOTS), FAR, ALU.is_gt, ALU.mult)
                dve.tensor_scalar(SUM, PLACE, 0.5, FAR, ALU.is_lt, ALU.mult)
                dve.drain()
                dve.tensor_tensor(AT, AT, OVER, ALU.add)
                dve.tensor_copy(drow[:, d, :, 2 * D], PRB)
                dve.tensor_copy(drow[:, d, :, 2 * D + 1], token1[:, bass.ds(g * UN, UN)])
                dve.drain()
                after(dve, S["drow_free"], g + 2)
                dve.tensor_tensor(slot[:, :], AT, SUM, ALU.add)
                dve.drain()
                dve.wait_ge(S["x1_copied"], g * UN + UN)
                dve.sem_inc(S["slot_ready"], 1)

            def route(g, d, before=True, later=True):
                if before:
                    choose(g - 1, 1 - d)
                    queue(g - 1, 1 - d)
                after(dve, S["drow_free"], g + 1)
                for u in range(UN):
                    block(g, d, u, later)

            route(0, 0, before=False)
            with dve.Fori(0, (NG - 3) // 2) as q:
                for i in range(2):
                    route(2 * q + (1 + i), 1 - i)
            route(NG - 2, 1)
            route(NG - 1, 0, later=False)
            choose(NG - 1, 0)
            queue(NG - 1, 0)
            dve.wait_ge(S["b2_in"], 16)

            with dve.Fori(0, N_EXP // 2) as q:
                for s in range(2):
                    dve.wait_ge(s_xs[s], 16 * q + 16)
                    dve.wait_ge(S["z_free"], 2 * q + (s + 1))
                    dve.tensor_scalar(tok_f[:, s, :], xs[:, s, :, 2 * D + 1], 0.5, FAR, ALU.is_lt, ALU.mult)
                    dve.drain()
                    dve.scalar_tensor_tensor(out=tok_f[:, s, :], in0=tok_f[:, s, :], scalar=-1.0,
                                             in1=xs[:, s, :, 2 * D + 1], op0=ALU.add, op1=ALU.add)
                    dve.drain()
                    dve.tensor_copy(tok[:, s, :], tok_f[:, s, :])
                    for t in range(NT):
                        rows = P if t < NT - 1 else SLOTS - (NT - 1) * P
                        z = z_sb[0:rows, t, :]
                        dve.wait_ge(S["y_ready"], 8 * q + (4 * s + t + 1))
                        dve.tensor_tensor(z, b(DOWN[t])[0:rows, 0:D], b2_all[0:rows, 2 * q + s, :], ALU.add
                                          ).then_inc(S["y_read"], 1)
                        dve.drain()
                        dve.tensor_scalar(z, z, xs[0:rows, s, t, 2 * D:2 * D + 1], None, ALU.mult)
                        dve.drain()
                        dve.tensor_tensor(odd[0:rows, 0, :], z, z, ALU.not_equal)
                        dve.tensor_scalar(odd[0:rows, 1, :], z, FLT_MAX, None, ALU.is_gt)
                        dve.tensor_scalar(odd[0:rows, 2, :], z, -FLT_MAX, None, ALU.is_lt)
                        for i in range(3):
                            dve.drain()
                            dve.copy_predicated(z, odd[0:rows, i, :], fills[0:rows, i, :])
                        dve.drain()
                        last = dve.tensor_tensor(z, z, xs[0:rows, s, t, 0:D], ALU.add)
                        last.then_inc(S["z_ready"], 1)
                    dve.drain()
                    dve.sem_inc(S["xs_free"], 1)

    return nc


_INS = ['x', 'src', 'dst', 'edge_weight', 'L0_gnn_weight_l', 'L0_gnn_bias_l', 'L0_gnn_weight_r', 'L0_gnn_bias_r',
        'L0_ffn_gate_w', 'L0_ffn_gate_b', 'L0_ffn_w1', 'L0_ffn_b1', 'L0_ffn_w2', 'L0_ffn_b2']


def kernel(**inputs):
    import numpy as _np
    import concourse.bacc as _bacc
    from concourse import mybir as _mybir
    from concourse.bass_utils import run_bass_kernel_spmd as _run

    nc = _bacc.Bacc("TRN2", target_bir_lowering=False, num_devices=1)
    arrays, args = {}, []
    for name in _INS:
        a = _np.ascontiguousarray(inputs[name])
        arrays[f"in_{name}_dram"] = a
        args.append(nc.dram_tensor(f"in_{name}_dram", a.shape, _mybir.dt.from_np(a.dtype), kind="ExternalInput").ap())
    h_rows = nc.dram_tensor("h_rows", (NB * P, D), _mybir.dt.float32, kind="Internal").ap()
    dispatch = nc.dram_tensor("dispatch", (N_EXP * ROWS_E, ROW), _mybir.dt.float32, kind="Internal").ap()
    out = nc.dram_tensor("out_0_dram", (N_NODES, D), _mybir.dt.float32, kind="ExternalOutput").ap()
    graph_moe(nc, *args, h_rows, dispatch, out)
    r = _run(nc, [arrays], core_ids=[0])
    return r.results[0]["out_0_dram"]
```

```python
import concourse.bass as bass
from concourse import mybir
from contextlib import ExitStack

P = 128
N_NODES, D, F_HID, N_EXP = 3125, 256, 1024, 8
N_EDGES = 53125
KD = D // P
KF = F_HID // P
NB = -(-N_NODES // P)
LAST = N_NODES - (NB - 1) * P
EP = 125
EC = N_EDGES // EP
SC = 5
CC = EC // SC
UN = 5
NG = NB // UN
PIECE = CC // NG
HALVES = ((0, (PIECE + 1) // 2), ((PIECE + 1) // 2, PIECE))
CAP = 512
NJ = CAP // P
SHORT = -(-NJ * LAST // P)
SHIFT = (NJ - SHORT) * P
REC = 6
ROUNDS = -(-(EP * CC + SHIFT) // CAP)
LW = NB * REC
SLOTS = 489
EVEN = SLOTS + SLOTS % 2
ROWS_E = -(-SLOTS // P) * P
NT = ROWS_E // P
SEAT = 5
SW = N_EXP * SEAT
EPS = 1e-5
FLT_MAX = 3.4028234663852886e38
LOW, HIGH = 15, 4080
FAR = 65536.0
assert EP * EC == N_EDGES and SC * CC == EC and NG * PIECE == CC and NG * UN == NB
assert NB * P < LOW + HIGH


def graph_moe(nc, x, src, dst, edge_weight, weight_l, bias_l, weight_r, bias_r,
              gate_w, gate_b, w1, b1, w2, b2, h_rows, norm_rows, out):
    f32, f32r, bf16, f16 = mybir.dt.float32, mybir.dt.float32r, mybir.dt.bfloat16, mybir.dt.float16
    i32, u32 = mybir.dt.int32, mybir.dt.uint32
    ALU = mybir.AluOpType
    ACT = mybir.ActivationFunctionType
    AX = mybir.AxisListType
    ctx = ExitStack()

    def sb(name, shape, dt):
        return ctx.enter_context(nc.sbuf_tensor(name, shape, dt))

    def pb(name, shape, dt=f32):
        return ctx.enter_context(nc.psum_tensor(name, shape, dt))

    where = {}

    def region(name, words):
        where[name] = -(-nc.sbuf_base // 32) * 32
        return sb(name, [P, words], mybir.dt.float32)

    def placed(name, over, at, words, dt):
        return nc.alloc_sbuf_tensor_at(name, [P, words], dt, offset=where[over] + 4 * at)[:, :]

    def sem(name):
        return ctx.enter_context(nc.semaphore(name))

    with ctx:
        ident = sb("ident", [P, P], f32)
        before = sb("before", [EP, EP], bf16)
        upto = sb("upto", [P, P], bf16)
        ones = sb("ones", [P, P], bf16)
        ones_row = sb("ones_row", [1, P], f32)
        run = sb("run", [EP, NB * CC], bf16)
        iota_block = sb("iota_block", [P, NB], f32)
        iota_node = sb("iota_node", [P, P], f32)
        iota_i = sb("iota_i", [P, max(CAP, ROWS_E)], i32)
        iota_rank = sb("iota_rank", [P, max(CAP, ROWS_E)], f16)
        rev = sb("rev", [P, N_EXP], f32)
        token1 = sb("token1", [P, NB], f32)
        valid = sb("valid", [P, NB], f32)
        fills = sb("fills", [P, 3, D], f32)
        token_i = sb("token_i", [P, 3, NB], i32)
        token_parts = sb("token_parts", [P, NB, 2], bf16)
        zero_bf = sb("zero_bf", [P, max(LW, NT * SW)], bf16)
        wlr = sb("wlr", [P, KD, 2 * D], f32)
        bias = sb("bias", [1, 2, D], f32)
        bias_sum = sb("bias_sum", [1, D], f32)
        gw = sb("gw", [P, KD, N_EXP], f32)
        gb = sb("gb", [1, N_EXP], f32)
        b1_rows = sb("b1_rows", [N_EXP * KF, P], f32)
        b1_cols = sb("b1_cols", [P, N_EXP * KF], f32)
        b2_all = sb("b2_all", [P, N_EXP, D], f32)
        late = region("late", 3 * KD * F_HID + KF * D)
        w1_raw = late[:, 0:KD * F_HID]
        w1_parts = placed("w1_parts", "late", KD * F_HID, 2 * KD * F_HID, f32r).rearrange(
            "p (i k f) -> p i k f", i=2, k=KD)
        w2_raw = late[:, 3 * KD * F_HID:]
        at_rank = late[0:EP, 0:PIECE * CAP // 2].bitcast(bf16).rearrange("p (c r) -> p c r", c=PIECE)
        at_blk = late[0:EP, PIECE * CAP // 2:PIECE * (CAP + LW) // 2].bitcast(bf16).rearrange(
            "p (c l) -> p c l", c=PIECE)
        nodes = region("nodes", NB * D)
        acc = nodes[:, :].rearrange("p (n d) -> p n d", d=D)
        z_sb = nodes[:, 2 * KF * D:2 * KF * D + NT * D].rearrange("p (t d) -> p t d", d=D)
        early = region("early", 2 * NB * D)
        parts = {}

        def place(name, at, words, dt=f32):
            parts[name] = (at, at + words)
            assert at + words <= 2 * NB * D
            return early[:, at:at + words] if dt == f32 else placed(name, "early", at, words, dt)

        xT = place("xT", 0, NB * D).rearrange("p (n d) -> p n d", d=D)
        h_sb = place("h", NB * D, NB * D).rearrange("p (n d) -> p n d", d=D)
        hot = place("hot", NB * D, UN * NJ * P).rearrange("p (n m) -> p n m", m=P)
        norm = place("norm", 0, 2 * UN * D).rearrange("p (s u d) -> p s u d", s=2, d=D)
        at_place = place("at_place", parts["hot"][1], UN * ROWS_E // 2).bitcast(bf16).rearrange(
            "p (u r) -> p u r", u=UN)
        full = place("full", 0, 2 * ROWS_E).rearrange("p (i t) -> p i t", i=2)
        hid = place("hid", parts["full"][1], 2 * KF * ROWS_E, f32r).rearrange("p (i f t) -> p i f t", i=2, f=KF)
        xnT = place("xnT", parts["hid"][1], 2 * KD * ROWS_E, f32r).rearrange("p (i k t) -> p i k t", i=2, k=KD)
        odd = place("odd", parts["xnT"][1], 6 * D).bitcast(i32).rearrange("p (i t d) -> p i t d", i=3, t=2)
        eps = sb("eps", [P, 1], f32)
        stats = sb("stats", [P, UN, 6], f32)
        moments = sb("moments", [P, NB, 2], f32)
        rstd = sb("rstd", [P, NB, 1], f32)
        moments2 = sb("moments2", [P, UN, 2], f32)
        rstd2 = sb("rstd2", [P, UN, 1], f32)
        xn = sb("xn", [P, UN, D], f32)
        xt = sb("xt", [P, UN, D], f32)
        xr = xn
        e_src = sb("e_src", [EP, EC], i32)
        e_dst = sb("e_dst", [EP, EC], i32)
        e_w = sb("e_w", [EP, EC], f32)
        landed = sb("landed", [P, UN * NJ * D], f32)
        fetched = landed[:, 0:UN * NJ * D].rearrange("p (n d) -> p n d", d=D)
        e_bits = landed[0:EP, 0:4 * EC].bitcast(i32).rearrange("p (i c) -> p i c", i=4)
        w_rest = landed[0:EP, 4 * EC:5 * EC]
        rank_top = sb("rank_top", [EP, 1], f32)
        rank_new = sb("rank_new", [1, 1], f32)
        rank_run = sb("rank_run", [1, 1], f32)
        rank_max = sb("rank_max", [1, 1], i32)
        blk = sb("blk", [EP, EC], f32)
        steps = region("steps", -(-(3 * NB * CC + REC * EC) // 2))
        count = steps[0:EP, 0:NB * CC]
        half = steps[0:EP, NB * CC:].bitcast(bf16)
        in_blk = half[:, 0:NB * CC]
        rec = half[:, NB * CC:NB * CC + REC * EC].rearrange("p (c i) -> p c i", i=REC)
        w2_parts = [placed(f"w2_parts_{over}", over, 0, 2 * KF * D, f32r).rearrange(
            "p (i f d) -> p i f d", i=2, f=KF) for over in ("steps", "nodes")]
        past = sb("past", [EP, CC], f32)
        total = sb("total", [EP, NB], bf16)
        rank = sb("rank", [EP, EC], f32)
        t_dst = sb("t_dst", [P, (SC + 1) * NB * NJ], f32)
        t_src = sb("t_src", [P, (SC + 1) * NB * NJ], f32)
        t_w = sb("t_w", [P, (SC + 1) * NB * NJ], f32)
        idx = sb("idx", [P, UN, NJ], u32)
        sm = sb("sm", [P, 6, UN, N_EXP], f32)
        sc1 = sb("sc1", [P, 5, UN], f32)
        hot_e = sb("hot_e", [P, UN, N_EXP], bf16)
        hot_sum = sb("hot_sum", [P, N_EXP], bf16)
        hot_new = sb("hot_new", [P, N_EXP], f32)
        entry = sb("entry", [P, UN, SEAT], bf16)
        entry_rest = sb("entry_rest", [P, UN], f32)
        entries = sb("entries", [P, UN, SW], bf16)
        seat_token = sb("seat_token", [P, N_EXP, NT], f32)
        seat_tmp = sb("seat_tmp", [P, N_EXP, NT], f32)
        seat_prob = sb("seat_prob", [P, N_EXP, NT], f32)
        seat_from = sb("seat_from", [P, N_EXP, NT], u32)
        seat_to = sb("seat_to", [P, N_EXP, NT], u32)
        xs = landed[:, 0:2 * NT * D].rearrange("p (s t d) -> p s t d", s=2, t=NT)
        row_from = sb("row_from", [P, 2, NT], u32)
        row_to = sb("row_to", [P, 2, NT], u32)
        prob = sb("prob", [P, 2, NT], f32)

        bank = [pb(f"bank{i}", [P, 512]) for i in range(4, 8)]
        ps_sort = pb("ps_sort", [P, 4, 512])

        def b(i):
            return ps_sort[:, i, :] if i < 4 else bank[i - 4][:, :]

        HL = (4, 5, 6, 4, 5)
        AG = (4, 5, 6, 4, 5)
        TP = (0, 1, 2, 3, 0)
        TP2 = (0, 1, 0, 1, 0)
        UP, DOWN = (2, 3, 6, 7, 2, 3, 6, 7), (4, 5)

        LG = [b(i)[:, 0:UN * N_EXP].rearrange("p (u e) -> p u e", e=N_EXP) for i in (2, 7)]
        POS = [b(i)[:, UN * N_EXP:2 * UN * N_EXP].rearrange("p (u e) -> p u e", e=N_EXP) for i in (2, 7)]
        SEATS = b(3)[:, 0:NT * SW]

        def used(banks, u):
            n = len(banks)
            return next(v for v in range(n + u - 1, -1, -1) if banks[v % n] == banks[u]) + 1

        names = (
            "const eps_ready bias_ready passed consts2 edges_in w_in bits_ready parts_ready wparts_ready "
            "total_ready base_ready var_ready std_ready xn_ready tp_ready xt_ready hp_ready h_evac h_stored "
            "calm block_ready row_ready xr_ready tail_ready rank_ready sort_used sort_done table_ready "
            "idx_ready hot_ready agg_done acc_added "
            "x2_ready tp2_ready xt2_ready lg_ready lmax_ready exp_ready hote_ready pos_ready place_ready "
            "seat_done seats_ready from_ready row_from_ready x1_out "
            "tpe_ready xn_hi xn_split hl_ready relu_done hid_split y_ready y_read z_ready w1_in w2_in w1_hi "
            "w2_hi w1_split w2_split b2_in "
            "more_in b1_t b1_ready top_ready top_t max_ready "
        ).split()
        S = {n: sem(n) for n in names}
        S["fetch"] = [sem(f"fetch{u}") for u in range(UN)]
        R = {n: sem("more_" + n) for n in ("rank_ready row_ready sort_used sort_done table_ready idx_ready hot_ready "
                                           "agg_done acc_added swept").split()}
        R["fetch"] = [sem(f"more_fetch{u}") for u in range(UN)]
        s_x = [sem(f"x_in{g}") for g in range(NG)]
        s_xs = [sem(f"xs_in{i}") for i in range(2)]
        s_rows = [sem(f"rows_stored{i}") for i in range(2)]
        s_out = [sem(f"out_tile{t}") for t in range(NT)]

        def after(eng, semaphore, value):
            eng.wait_ge(semaphore, value)
            eng.sem_inc(S["passed"], 1)

        def record_rows(eng, s, g, c0, c1):
            return eng.tensor_tensor(
                at_blk[:, c0:c1, :].rearrange("p c (b i) -> p c b i", i=REC),
                in_blk[:, :].rearrange("p (b c) -> p c b", c=CC)[:, bass.ds(g * PIECE + c0, c1 - c0), :, None]
                .broadcast_to([EP, c1 - c0, NB, REC]),
                rec[:, bass.ds(s * CC + g * PIECE + c0, c1 - c0), None, :].broadcast_to([EP, c1 - c0, NB, REC]),
                ALU.mult)

        def more_rounds(eng, free, body):
            eng.wait_ge(S["max_ready"], SC)
            largest = eng.value_load(rank_max[0:1, 0:1], min_val=0, max_val=EP * CC + SHIFT)
            with eng.If(largest > CAP):
                eng.wait_ge(S["calm"], 1)
                for name, n in free:
                    eng.sem_inc(R[name], n)
                with eng.Fori(1, ROUNDS) as r:
                    with eng.If(largest > r * CAP):
                        with eng.Fori(0, SC) as s:
                            k = (r - 1) * SC + s
                            body(s, k)
                            eng.wait_ge(R["swept"], k + 1)
                            eng.sem_inc(S["passed"], 1)

        block = ctx.enter_context(nc.Block())

        @block.sync
        def _(sp):
            def load_x(g):
                n = UN if g < NG - 1 else UN - 1
                sp.dma_start(acc[:, g * UN:g * UN + n, :], x[g * UN * P:(g * UN + n) * P, :].rearrange(
                    "(n p) d -> p n d", p=P)).then_inc(s_x[g], 16)

            load_x(0)
            for rows, edge in ((e_src, src), (e_dst, dst), (e_w, edge_weight)):
                sp.dma_start(rows[:, :], edge.rearrange("(p c) -> p c", c=EC)).then_inc(S["edges_in"], 16)
            for g in range(1, NG):
                load_x(g)
            sp.wait_ge(S["consts2"], 1)
            sp.dma_start(acc[0:LAST, NB - 1, :], x[(NB - 1) * P:N_NODES, :]).then_inc(s_x[NG - 1], 16)
            for k in range(KD):
                sp.dma_start(wlr[:, k, D:2 * D], weight_r[k * P:(k + 1) * P, :]).then_inc(S["more_in"], 16)
            sp.dma_start(bias[:, 0, :], bias_l[None, :]).then_inc(S["more_in"], 16)
            sp.dma_start(bias[:, 1, :], bias_r[None, :]).then_inc(S["more_in"], 16)
            sp.dma_start(gw[:, :, :], gate_w.rearrange("(k p) e -> p k e", p=P)).then_inc(S["more_in"], 16)
            sp.dma_start(gb[:, :], gate_b[None, :]).then_inc(S["more_in"], 16)
            sp.dma_start(b1_rows[:, :], b1.rearrange("e (f p) -> (e f) p", p=P)).then_inc(S["more_in"], 16)
            with sp.Fori(0, NG) as g:
                sp.wait_ge(S["h_evac"], g * UN + 2 * UN)
                sp.dma_start(h_rows[bass.ds(g * (UN * P), UN * P), :].rearrange("(n p) d -> p n d", p=P),
                             h_sb[:, bass.ds(g * UN, UN), :]).then_inc(S["h_stored"], 16)
            sp.dma_start(b2_all[:, :, :].rearrange("p e d -> p (e d)"),
                         b2.rearrange("e d -> (e d)")[None, :].broadcast_to([P, N_EXP * D])
                         ).then_inc(S["b2_in"], 16)
            sp.wait_ge(S["table_ready"], SC)
            sp.wait_ge(S["max_ready"], SC)
            sp.wait_ge(S["tail_ready"], 1)

            def load_w1(e):
                sp.dma_start(w1_raw.rearrange("p (k f) -> p k f", k=KD),
                             w1[bass.ds(e, 1)].rearrange("a (k p) f -> p (a k) f", p=P)).then_inc(S["w1_in"], 16)

            def load_w2(e):
                sp.dma_start(w2_raw.rearrange("p (f d) -> p f d", f=KF),
                             w2[bass.ds(e, 1)].rearrange("a (f p) d -> p (a f) d", p=P)).then_inc(S["w2_in"], 16)

            load_w1(0)
            load_w2(0)
            for g in range(NG):
                n = UN if g < NG - 1 else UN - 1
                sp.wait_ge(S["x2_ready"], (g + 1) * UN)
                sp.dma_start(norm_rows[g * UN * P:(g + 1) * UN * P, :].rearrange("(n p) d -> p n d", p=P),
                             norm[:, g % 2, :, :]).then_inc(s_rows[g % 2], 16)
                sp.dma_start(out[g * UN * P:(g * UN + n) * P, :].rearrange("(n p) d -> p n d", p=P),
                             acc[:, g * UN:g * UN + n, :]).then_inc(S["x1_out"], 16)
            sp.dma_start(out[(NB - 1) * P:N_NODES, :], acc[0:LAST, NB - 1, :]).then_inc(S["x1_out"], 16)
            sp.wait_ge(s_xs[0], 16 * NT)
            with sp.Fori(0, N_EXP - 1) as e:
                sp.wait_ge(S["w1_split"], e + 1)
                load_w1(e + 1)
                sp.wait_ge(S["w2_split"], e + 1)
                load_w2(e + 1)

        @block.gpsimd
        def _(pool):
            pool.memset(acc[:, NB - 1, :], 0.0).then_inc(S["consts2"], 1)
            pool.memset(ident[:, :], 0.0)
            pool.memset(before[:, :], 1.0)
            pool.memset(upto[:, :], 1.0)
            pool.iota(iota_block[:, :], pattern=[[1, NB]], base=0, channel_multiplier=0,
                      allow_small_or_imprecise_dtypes=True)
            pool.iota(iota_node[:, :], pattern=[[1, P]], base=0, channel_multiplier=0,
                      allow_small_or_imprecise_dtypes=True)
            pool.iota(iota_i[:, :], pattern=[[1, max(CAP, ROWS_E)]], base=1, channel_multiplier=0)
            pool.iota(rev[:, :], pattern=[[-1, N_EXP]], base=N_EXP, channel_multiplier=0,
                      allow_small_or_imprecise_dtypes=True)
            pool.iota(token_i[:, 0, :], pattern=[[P, NB]], base=1, channel_multiplier=1)
            pool.iota(token1[:, :], pattern=[[P, NB]], base=1, channel_multiplier=1,
                      allow_small_or_imprecise_dtypes=True)
            pool.memset(ones[:, :], 1.0)
            pool.memset(ones_row[:, :], 1.0)
            pool.memset(run[:, :], 1.0)
            pool.memset(fills[:, 0, :], 0.0)
            pool.memset(fills[:, 1, :], 1e4)
            pool.memset(fills[:, 2, :], -1e4)
            pool.memset(hot_sum[:, :], 0.0)
            pool.drain()
            pool.memset(run[:, :].rearrange("p (b c) -> p b c", c=CC)[:, :, 0:1], 0.0)
            pool.affine_select(out=ident[:, :], in_=ident[:, :], compare_op=ALU.not_equal, fill=1.0,
                               base=0, pattern=[[-1, P]], channel_multiplier=1)
            pool.affine_select(out=before[:, :], in_=before[:, :], compare_op=ALU.is_gt, fill=0.0,
                               base=0, pattern=[[1, EP]], channel_multiplier=-1)
            pool.affine_select(out=upto[:, :], in_=upto[:, :], compare_op=ALU.is_ge, fill=0.0,
                               base=0, pattern=[[1, P]], channel_multiplier=-1)
            pool.drain()
            pool.sem_inc(S["const"], 1)
            pool.wait_ge(S["edges_in"], 48)
            pool.tensor_copy(rec[:, :, 3], e_w[:, :])
            pool.drain()
            pool.tensor_tensor(w_rest, e_w[:, :], rec[:, :, 3], ALU.subtract)
            pool.drain()
            pool.tensor_copy(rec[:, :, 4], w_rest)
            pool.drain()
            pool.tensor_tensor(rec[:, :, 5], w_rest, rec[:, :, 4], ALU.subtract
                               ).then_inc(S["wparts_ready"], 1)
            def rows(g):
                for c0, c1 in HALVES:
                    after(pool, S["sort_used"], 2 * g + (1 if c0 == 0 else 2))
                    record_rows(pool, 0, g, c0, c1).then_inc(S["row_ready"], 1)

            pool.drain()
            pool.wait_ge(S["block_ready"], 1)
            pool.wait_ge(S["parts_ready"], 1)
            with pool.Fori(0, NG) as g:
                rows(g)

            def gathers(Q, n, us=range(UN), short=False):
                for u in us:
                    after(pool, Q["idx_ready"], n * UN + (u + 1))
                    for j in range(SHORT if short and u == UN - 1 else NJ):
                        pool.indirect_dma_start(
                            fetched[:, u * NJ + j, :], None, h_rows,
                            bass.IndirectOffsetOnAxis(ap=idx[:, u, j:j + 1], axis=0)).then_inc(Q["fetch"][u], 16)

            pool.wait_ge(S["h_stored"], NG * 16)
            with pool.Fori(0, SC - 1) as s:
                with pool.Fori(0, NG - 1) as g:
                    gathers(S, g + s * NG)
                gathers(S, s * NG + (NG - 1), short=True)

            def more(s, k):
                with pool.Fori(0, NG) as g:
                    gathers(R, k * NG + g)

            more_rounds(pool, (), more)
            with pool.Fori(0, NG - 1) as g:
                gathers(S, g + (SC - 1) * NG)
            gathers(S, SC * NG - 1, short=True)

            def split_w1(e):
                after(pool, S["w1_hi"], e + 1)
                pool.tensor_tensor(w1_parts[:, 1, :, :].rearrange("p k f -> p (k f)"), w1_raw,
                                   w1_parts[:, 0, :, :].rearrange("p k f -> p (k f)").bitcast(f32), ALU.subtract
                                   ).then_inc(S["w1_split"], 1)

            def split_w2(e, s):
                after(pool, S["w2_hi"], e + 1)
                pool.tensor_tensor(w2_parts[s][:, 1, :, :].rearrange("p f d -> p (f d)"), w2_raw,
                                   w2_parts[s][:, 0, :, :].rearrange("p f d -> p (f d)").bitcast(f32), ALU.subtract
                                   ).then_inc(S["w2_split"], 1)

            def fetch_rows(e, s):
                after(pool, S["row_from_ready"], e + 1)
                after(pool, S["tpe_ready"], 2 * e + 2)
                for t in range(NT):
                    pool.indirect_dma_start(
                        xs[:, s, t, :], None, norm_rows,
                        bass.IndirectOffsetOnAxis(ap=row_from[:, s, t:t + 1], axis=0)).then_inc(s_xs[s], 16)

            split_w1(0)
            for i in range(2):
                pool.wait_ge(s_rows[i], 16 * len(range(i, NG, 2)))
            fetch_rows(0, 0)
            split_w2(0, 0)
            fetch_rows(1, 1)
            pool.wait_ge(S["x1_out"], 16 * (NG + 1))

            def send(e, s, h):
                after(pool, S["z_ready"], 2 * e + (h + 1))
                for t in (2 * h, 2 * h + 1):
                    rows = P if t < NT - 1 else SLOTS - (NT - 1) * P
                    pool.indirect_dma_start(
                        out, bass.IndirectOffsetOnAxis(ap=row_to[0:rows, s, t:t + 1], axis=0),
                        z_sb[0:rows, t, :], None,
                        bounds_check=N_NODES - 1, oob_is_err=False, compute_op=ALU.add).then_inc(s_out[t], 16)

            def expert(e, s):
                fetch_rows(e + 1, 1 - s)
                send(e - 1, 1 - s, 0)
                split_w1(e + 1)
                send(e - 1, 1 - s, 1)
                split_w2(e + 1, 1 - s)

            split_w1(1)
            split_w2(1, 1)
            with pool.Fori(0, (N_EXP - 2) // 2) as q:
                for s in range(2):
                    expert(2 * q + (1 + s), 1 - s)
            for e in range(N_EXP - 2, N_EXP):
                for h in range(2):
                    send(e, e % 2, h)
            for t in range(NT):
                pool.wait_ge(s_out[t], 16 * N_EXP)

        @block.scalar
        def _(act):
            for k in range(KD):
                act.dma_start(wlr[:, k, 0:D], weight_l[k * P:(k + 1) * P, :]).then_inc(S["w_in"], 16)
            act.sem_inc(S["xt_ready"], UN)
            act.sem_inc(S["h_evac"], UN)

            def root(i, mom, dev):
                act.wait_ge(S["var_ready"], i + 1)
                act.activation(dev, mom[:, :, 1:2], ACT.Sqrt, bias=eps[:, 0:1]).then_inc(S["std_ready"], 1)

            act.wait_ge(S["eps_ready"], 1)
            root(0, moments[:, 0:UN, :], rstd[:, 0:UN, :])
            for g in range(NG):
                for t in range(g * UN, (g + 1) * UN):
                    act.wait_ge(S["tp_ready"], UN + t + 1)
                    act.activation(xT[:, t, :], b(TP[t % UN])[:, 0:D], ACT.Copy).then_inc(S["xt_ready"], 1)
                if g + 1 < NG:
                    root(g + 1, moments[:, (g + 1) * UN:(g + 2) * UN, :], rstd[:, (g + 1) * UN:(g + 2) * UN, :])
                if g == 0:
                    act.wait_ge(S["bits_ready"], 1)
                    act.activation(blk[:, :], e_bits[:, 0, :], ACT.Copy)
                    for i in range(3):
                        act.activation(rec[:, :, i], e_bits[:, i + 1, :], ACT.Copy)
                    act.drain()
                    act.sem_inc(S["parts_ready"], 1)
                for t in range(g * UN, (g + 1) * UN):
                    act.wait_ge(S["hp_ready"], UN + t + 1)
                    act.activation(h_sb[:, t, :], b(HL[t % UN])[:, 0:D], ACT.Copy).then_inc(S["h_evac"], 1)

            act.wait_ge(S["b1_t"], 1)
            act.activation(b1_cols[:, :], b(7)[:, 0:N_EXP * KF], ACT.Copy).then_inc(S["b1_ready"], 1)

            def copy_idx(Q, at, n, u):
                act.wait_ge(Q["agg_done"], n * UN + (u + 1))
                act.activation(idx[:, u, :], t_dst[:, bass.ds(at * (UN * NJ) + u * NJ, NJ)], ACT.Copy
                               ).then_inc(Q["idx_ready"], 1)

            act.wait_ge(S["table_ready"], 1)
            with act.Fori(0, NG) as g:
                for u in range(UN):
                    copy_idx(S, g, g, u)
                    act.activation(xr[:, u, :], xT[:, g * UN + u, :], ACT.Copy).then_inc(S["xr_ready"], 1)
            with act.Fori(1, SC - 1) as s:
                act.wait_ge(S["table_ready"], s + 1)
                with act.Fori(0, NG) as g:
                    for u in range(UN):
                        copy_idx(S, s * NG + g, s * NG + g, u)

            def more(s, k):
                act.wait_ge(R["table_ready"], k + 1)
                with act.Fori(0, NG) as g:
                    for u in range(UN):
                        copy_idx(R, g + SC * NG, k * NG + g, u)

            more_rounds(act, (), more)
            act.wait_ge(S["table_ready"], SC)
            for u in range(UN):
                copy_idx(S, (SC - 1) * NG, (SC - 1) * NG, u)

            def exponent(g):
                act.wait_ge(S["lmax_ready"], g + 1)
                act.activation(sm[:, 1, :, :], sm[:, 0, :, :], ACT.Exp).then_inc(S["exp_ready"], 1)

            def turned(g, u):
                act.wait_ge(S["tp2_ready"], g * UN + (u + 1))
                act.wait_ge(S["lg_ready"], g * UN + (u + 1))
                act.activation(xt[:, u, :], b(TP2[u])[:, 0:D], ACT.Copy).then_inc(S["xt2_ready"], 1)

            def step(g, u):
                if g < NG - 1:
                    copy_idx(S, (SC - 1) * NG + g + 1, (SC - 1) * NG + g + 1, u)
                if u > 0 or g > 0:
                    turned(g if u > 0 else g - 1, (u - 1) % UN)
                root(g * UN + (NG + u), moments2[:, u:u + 1, :], rstd2[:, u:u + 1, :])
                if u == 1 and g > 0:
                    exponent(g - 1)

            for g in range(NG):
                for u in range(UN):
                    step(g, u)
            turned(NG - 1, UN - 1)
            exponent(NG - 1)

            def round_w1(e):
                act.wait_ge(S["w1_in"], 16 * e + 16)
                act.wait_ge(S["hl_ready"], 8 * e + KF)
                act.activation(w1_parts[:, 0, :, :].rearrange("p k f -> p (k f)"), w1_raw, ACT.Copy
                               ).then_inc(S["w1_hi"], 1)

            def round_w2(e, s, again=True):
                act.wait_ge(S["w2_in"], 16 * e + 16)
                if again:
                    act.wait_ge(S["y_ready"], 2 * e - 2)
                act.activation(w2_parts[s][:, 0, :, :].rearrange("p f d -> p (f d)"), w2_raw, ACT.Copy
                               ).then_inc(S["w2_hi"], 1)

            round_w1(0)
            round_w2(0, 0, again=False)

            def row_index(e, s, again=True):
                if again:
                    act.wait_ge(s_xs[s], 32 * (e - s))
                act.activation(row_from[:, s, :], seat_from[:, bass.ds(e, 1), :], ACT.Copy
                               ).then_inc(S["row_from_ready"], 1)

            act.wait_ge(S["from_ready"], 1)
            row_index(0, 0, again=False)
            row_index(1, 1, again=False)
            act.wait_ge(S["x1_out"], 16 * (NG + 1))

            def rows_hi(e):
                for k in range(KD):
                    act.wait_ge(S["tpe_ready"], 2 * e + (2 * KD + k + 1))
                    act.activation(xnT[:, 0, k, :], b(k), ACT.Copy).then_inc(S["xn_hi"], 1)

            def hidden(e):
                for f in range(KF):
                    act.wait_ge(S["hl_ready"], 8 * e + (KF + f + 1))
                    act.wait_ge(S["hid_split"], 8 * e + (f + 1))
                    bias_f = b1_cols[:, bass.ds(8 * e + f, 1)]
                    act.activation(hid[:, 0, f, 0:EVEN], b(UP[f])[:, 0:EVEN], ACT.Relu, bias=bias_f)
                    act.activation(full[:, f % 2, 0:EVEN], b(UP[f])[:, 0:EVEN], ACT.Relu, bias=bias_f
                                   ).then_inc(S["relu_done"], 1)

            def expert(e, s, again=True):
                if again:
                    row_index(e + 1, 1 - s)
                hidden(e)
                round_w1(e + 1)
                rows_hi(e + 1)
                round_w2(e + 1, 1 - s, again)

            rows_hi(0)
            expert(0, 0, again=False)
            with act.Fori(0, (N_EXP - 2) // 2) as q:
                for s in range(2):
                    expert(2 * q + (1 + s), 1 - s)
            hidden(N_EXP - 1)

        @block.tensor
        def _(pe):
            pe.sem_inc(S["agg_done"], UN)
            pe.sem_inc(S["tp_ready"], UN)

            pe.sem_inc(S["hp_ready"], UN)
            pe.sem_inc(S["hl_ready"], KF)
            pe.sem_inc(S["tpe_ready"], 2 * KD)
            pe.sem_inc(S["sort_used"], 2)
            pe.sem_inc(S["lg_ready"], UN)
            pe.wait_ge(S["const"], 1)
            pe.wait_ge(S["w_in"], 16 * KD)

            def project(g):
                for u in range(UN):
                    t = g * UN + u
                    pe.wait_ge(S["xn_ready"], t + 1)
                    pe.wait_ge(S["xt_ready"], g * UN + used(TP, u))
                    for k in range(KD):
                        last = pe.transpose(b(TP[u])[:, k * P:(k + 1) * P], xn[:, u, k * P:(k + 1) * P], ident[:, :])
                    last.then_inc(S["tp_ready"], 1)
                for u in range(UN):
                    t = g * UN + u
                    pe.wait_ge(S["xt_ready"], UN + t + 1)
                    pe.wait_ge(S["h_evac"], g * UN + used(HL, u))
                    for k in range(KD):
                        last = pe.matmul(b(HL[u])[:, 0:D], lhsT=xT[:, t, k * P:(k + 1) * P],
                                         rhs=wlr[:, k, 0:D], start=(k == 0), stop=(k == KD - 1))
                    last.then_inc(S["hp_ready"], 1)

            def base(s):
                pe.wait_ge(S["total_ready"], s + 1)
                pe.matmul(b(7)[0:EP, 0:NB], lhsT=before[:, :], rhs=total[:, :], start=True, stop=True
                          ).then_inc(S["base_ready"], 1)

            def open_sort():
                for j in range(NJ):
                    pe.matmul(ps_sort[:, j, 0:LW], lhsT=zero_bf[0:EP, 0:P], rhs=zero_bf[0:EP, 0:LW],
                              start=True, stop=False)

            def close_sort(Q):
                for j in range(NJ):
                    last = pe.matmul(ps_sort[:, j, 0:LW], lhsT=zero_bf[0:EP, 0:P], rhs=zero_bf[0:EP, 0:LW],
                                     start=False, stop=True)
                last.then_inc(Q["sort_done"], 1)

            def sort_piece(Q, m):
                for i, (c0, c1) in enumerate(HALVES):
                    pe.wait_ge(Q["row_ready"], 2 * m + (i + 1))
                    for c in range(c0, c1):
                        pe.wait_ge(Q["rank_ready"], m * PIECE + (c + 1))
                        for j in range(NJ):
                            last = pe.matmul(ps_sort[:, j, 0:LW], lhsT=at_rank[:, c, j * P:(j + 1) * P],
                                             rhs=at_blk[:, c, :], start=False, stop=False)
                    last.then_inc(Q["sort_used"], 1)

            def aggregate(Q, n, us=range(UN), own=False, at=None, short=False):
                for u in us:
                    pe.wait_ge(Q["acc_added"], n * UN + used(AG, u))
                    if own:
                        pe.wait_ge(S["xr_ready"], n * UN + (u + 1))
                        for k in range(KD):
                            pe.matmul(b(AG[u])[:, 0:D], lhsT=xr[:, u, k * P:(k + 1) * P],
                                      rhs=wlr[:, k, D:2 * D], start=(k == 0), stop=False)
                        pe.matmul(b(AG[u])[:, 0:D], lhsT=ones_row[:, :], rhs=bias_sum[:, :],
                                  start=False, stop=False)
                    tiles = SHORT if short and u == UN - 1 else NJ
                    if at is None or u < UN - 1:
                        pe.wait_ge(Q["fetch"][u], n * (16 * NJ) + 16 * NJ)
                    else:
                        s, g = at
                        pe.wait_ge(Q["fetch"][u], s * (16 * (NG * NJ - NJ + SHORT)) + g * (16 * NJ) + 16 * tiles)
                    pe.wait_ge(Q["hot_ready"], n * (UN * NJ) + (u + 1) * NJ)
                    for j in range(tiles):
                        last = pe.matmul(b(AG[u])[:, 0:D], lhsT=hot[:, u * NJ + j, :],
                                         rhs=fetched[:, u * NJ + j, :],
                                         start=(j == 0 and not own), stop=(j == tiles - 1))
                    last.then_inc(Q["agg_done"], 1)

            project(0)
            project(1)
            base(0)
            for g in range(2, NG):
                project(g)
            open_sort()
            for g in range(NG):
                sort_piece(S, g)
            close_sort(S)

            def top(s):
                pe.wait_ge(S["top_ready"], s + 1)
                pe.transpose(b(7)[0:1, 0:EP], rank_top[:, :], ident[0:EP, 0:EP]).then_inc(S["top_t"], 1)

            top(0)
            pe.wait_ge(S["max_ready"], 1)
            pe.wait_ge(S["more_in"], 16 * (KD + 5))
            pe.transpose(b(7)[:, 0:N_EXP * KF], b1_rows[:, :], ident[0:N_EXP * KF, 0:N_EXP * KF]
                         ).then_inc(S["b1_t"], 1)
            pe.wait_ge(S["bias_ready"], 1)
            pe.wait_ge(S["b1_ready"], 1)

            def sum_and_sort(s, own):
                aggregate(S, s * NG, range(0, 2), own)
                base(s + 1)
                aggregate(S, s * NG, range(2, UN), own, (s, 0))
                top(s + 1)
                pe.wait_ge(S["table_ready"], s + 1)
                open_sort()
                sort_piece(S, (s + 1) * NG)
                with pe.Fori(1, NG - 1) as g:
                    aggregate(S, g + s * NG, own=own, at=(s, g))
                    sort_piece(S, g + (s + 1) * NG)
                sort_piece(S, (s + 1) * NG + (NG - 1))
                close_sort(S)
                aggregate(S, s * NG + (NG - 1), own=own, at=(s, NG - 1), short=True)

            sum_and_sort(0, True)
            with pe.Fori(1, SC - 1) as s:
                sum_and_sort(s, False)

            def more(s, k):
                open_sort()
                with pe.Fori(0, NG) as g:
                    sort_piece(R, k * NG + g)
                close_sort(R)
                with pe.Fori(0, NG) as g:
                    aggregate(R, k * NG + g)

            more_rounds(pe, (("agg_done", UN), ("sort_used", 2)), more)

            def turn(g, d, u):
                pe.wait_ge(S["x2_ready"], g * UN + (u + 1))
                pe.wait_ge(S["xt2_ready"], g * UN + used(TP2, u))
                for k in range(KD):
                    last = pe.transpose(b(TP2[u])[:, k * P:(k + 1) * P],
                                        norm[:, d, u, k * P:(k + 1) * P], ident[:, :])
                last.then_inc(S["tp2_ready"], 1)

            def logits(g, d, u):
                pe.wait_ge(S["xt2_ready"], g * UN + (UN + u + 1))
                for k in range(KD):
                    pe.matmul(LG[d][:, u, :], lhsT=xt[:, u, k * P:(k + 1) * P], rhs=gw[:, k, :],
                              start=(k == 0), stop=False)
                pe.matmul(LG[d][:, u, :], lhsT=ones_row[:, :], rhs=gb[:, :], start=False, stop=True
                          ).then_inc(S["lg_ready"], 1)

            def position(g, d):
                pe.wait_ge(S["hote_ready"], g + 1)
                for u in range(UN):
                    pe.matmul(POS[d][:, u, :], lhsT=ones[:, :], rhs=hot_sum[:, :], start=True, stop=False)
                    for v in range(u):
                        pe.matmul(POS[d][:, u, :], lhsT=ones[:, :], rhs=hot_e[:, v, :], start=False, stop=False)
                    last = pe.matmul(POS[d][:, u, :], lhsT=upto[:, :], rhs=hot_e[:, u, :], start=False, stop=True)
                last.then_inc(S["pos_ready"], 1)

            def seats(g):
                pe.wait_ge(S["place_ready"], g + 1)
                for u in range(UN):
                    for j in range(NT):
                        last = pe.matmul(SEATS[:, j * SW:(j + 1) * SW], lhsT=at_place[:, u, j * P:(j + 1) * P],
                                         rhs=entries[:, u, :], start=False, stop=False)
                last.then_inc(S["seat_done"], 1)

            def no_seats(start, stop):
                return pe.matmul(SEATS, lhsT=zero_bf[:, 0:P], rhs=zero_bf[:, 0:NT * SW], start=start, stop=stop)

            no_seats(True, False)
            for t in range(NB + 2):
                g, u = t // UN, t % UN
                if t < NB:
                    aggregate(S, g + (SC - 1) * NG, (u,), at=(SC - 1, g), short=(g == NG - 1))
                if 1 <= t <= NB:
                    turn((t - 1) // UN, (t - 1) // UN % 2, (t - 1) % UN)
                if t >= 2:
                    logits((t - 2) // UN, (t - 2) // UN % 2, (t - 2) % UN)
                if 0 < g < NG and u == 3:
                    position(g - 1, (g - 1) % 2)
                if 0 < g < NG and u == 4:
                    seats(g - 1)
            position(NG - 1, 0)
            seats(NG - 1)
            no_seats(False, True).then_inc(S["seats_ready"], 1)

            def split_product(outp, left, right, first, last):
                pe.matmul(outp, lhsT=left(0), rhs=right(0), start=first, stop=False)
                pe.matmul(outp, lhsT=left(0), rhs=right(1), start=False, stop=False)
                return pe.matmul(outp, lhsT=left(1), rhs=right(0), start=False, stop=last)

            def turn_rows(e, s):
                pe.wait_ge(s_xs[s], 32 * (e - s) + 64)
                pe.wait_ge(S["xn_split"], 2 * e + 2)
                for k in range(KD):
                    for t in range(NT):
                        last = pe.transpose(b(k)[:, t * P:(t + 1) * P], xs[:, s, t, k * P:(k + 1) * P],
                                            ident[:, :])
                    last.then_inc(S["tpe_ready"], 1)

            def up(e):
                pe.wait_ge(S["w1_split"], e + 1)
                pe.wait_ge(S["xn_split"], 2 * e + 4)
                for f in range(KF):
                    pe.wait_ge(S["relu_done"], 8 * e + used(UP, f))
                    for k in range(KD):
                        last = split_product(b(UP[f])[:, 0:EVEN], lambda i: w1_parts[:, i, k, f * P:(f + 1) * P],
                                             lambda i: xnT[:, i, k, 0:EVEN], k == 0, k == KD - 1)
                    last.then_inc(S["hl_ready"], 1)

            def down(e, s, h):
                pe.wait_ge(S["w2_split"], e + 1)
                pe.wait_ge(S["y_read"], 2 * e + (h + 1))
                for i in range(2):
                    t = 2 * h + i
                    for f in range(KF):
                        if t == 0:
                            pe.wait_ge(S["hid_split"], 8 * e + (f + 3))
                        last = split_product(b(DOWN[h])[:, i * D:(i + 1) * D],
                                             lambda j: hid[:, j, f, t * P:(t + 1) * P],
                                             lambda j: w2_parts[s][:, j, f, :], f == 0, f == KF - 1)
                last.then_inc(S["y_ready"], 1)

            def expert(e, s):
                up(e)
                turn_rows(e + 1, 1 - s)
                for h in range(2):
                    down(e, s, h)

            turn_rows(0, 0)
            expert(0, 0)
            with pe.Fori(0, (N_EXP - 2) // 2) as q:
                for s in range(2):
                    expert(2 * q + (1 + s), 1 - s)
            up(N_EXP - 1)
            for h in range(2):
                down(N_EXP - 1, 1, h)

        @block.vector
        def _(dve):
            dve.sem_inc(S["acc_added"], UN)
            dve.sem_inc(S["xt2_ready"], UN)
            dve.sem_inc(S["xn_split"], 2)
            dve.sem_inc(S["relu_done"], KF)
            dve.sem_inc(S["hid_split"], 2)
            dve.sem_inc(S["y_read"], 2)
            dve.memset(zero_bf[:, :], 0.0)
            dve.memset(rank_run[:, :], 0.0)
            dve.memset(eps[:, :], EPS).then_inc(S["eps_ready"], 1)
            blkT = in_blk[:, :].rearrange("p (b c) -> p b c", c=CC)
            countT = count[:, :].rearrange("p (b c) -> p b c", c=CC)

            def block_hot(s):
                dve.tensor_tensor(blkT, blk[:, None, bass.ds(s * CC, CC)].broadcast_to([EP, NB, CC]),
                                  iota_block[0:EP, :, None].broadcast_to([EP, NB, CC]), ALU.is_equal)
                dve.drain()

            def running_count(s):
                dve.tensor_tensor_scan(count[:, :], run[:, :], in_blk[:, :], 0.0, ALU.mult, ALU.add)
                dve.drain()
                dve.tensor_copy(total[:, :], countT[:, :, CC - 1]).then_inc(S["total_ready"], 1)

            def place_count(s):
                dve.wait_ge(S["base_ready"], s + 1)
                dve.tensor_tensor(countT, countT, b(7)[0:EP, 0:NB, None].broadcast_to([EP, NB, CC]), ALU.add)
                dve.drain()
                dve.tensor_scalar(past[:, :], countT[:, NB - 1, :], float(SHORT * P), float(SHIFT),
                                  ALU.is_gt, ALU.mult)
                dve.drain()
                dve.tensor_tensor(countT[:, NB - 1, :], countT[:, NB - 1, :], past[:, :], ALU.add)
                dve.drain()
                dve.tensor_tensor(count[:, :], count[:, :], in_blk[:, :], ALU.mult)
                dve.drain()
                dve.tensor_reduce(rank[:, bass.ds(s * CC, CC)], count[:, :].rearrange("p (b c) -> p c b", c=CC),
                                  AX.X, ALU.add)
                dve.drain()

            def build_piece(Q, s, g, m, rows=True):
                for c0, c1 in HALVES:
                    dve.wait_ge(Q["sort_used"], 2 * m + (1 if c0 == 0 else 2))
                    if rows:
                        record_rows(dve, s, g, c0, c1).then_inc(Q["row_ready"], 1)
                    for c in range(c0, c1):
                        dve.tensor_scalar(at_rank[:, c, :], iota_rank[0:EP, 0:CAP],
                                          rank[:, bass.ds(s * CC + g * PIECE + c, 1)], None,
                                          ALU.is_equal).then_inc(Q["rank_ready"], 1)

            def take_table(Q, at, k):
                dve.wait_ge(Q["sort_done"], k + 1)

                def parts_of(i, n):
                    return ps_sort[:, 0:NJ, 0:LW].rearrange("p j (b i) -> p j b i", i=REC)[:, :, :, i:i + n]

                def table(t):
                    return t[:, bass.ds(at * (NB * NJ), NB * NJ)].rearrange("p (b j) -> p j b", j=NJ)

                dve.tensor_copy(table(t_src), parts_of(0, 1)[:, :, :, 0])
                dve.tensor_reduce(table(t_dst), parts_of(1, 2), AX.X, ALU.add)
                dve.tensor_reduce(table(t_w), parts_of(3, 3), AX.X, ALU.add)
                dve.drain()
                dve.sem_inc(Q["table_ready"], 1)

            def weighted_hot(Q, at_n, n, us=range(UN)):
                for u in us:
                    dve.wait_ge(Q["agg_done"], n * UN + (u + 1))
                    for j in range(NJ):
                        at = at_n * (UN * NJ) + (u * NJ + j)
                        dve.tensor_scalar(hot[:, u * NJ + j, :], iota_node[:, :], t_src[:, bass.ds(at, 1)],
                                          t_w[:, bass.ds(at, 1)], ALU.is_equal, ALU.mult
                                          ).then_inc(Q["hot_ready"], 1)

            def add_and_next(n, g, us=range(UN)):
                for u in us:
                    add_blocks(S, n, g, (u,))
                    weighted_hot(S, n + 1, n + 1, (u,))

            def add_blocks(Q, n, g, us=range(UN)):
                for u in us:
                    dve.wait_ge(Q["agg_done"], n * UN + (UN + u + 1))
                    dve.tensor_tensor(acc[:, g * UN + u, :], acc[:, g * UN + u, :], b(AG[u])[:, 0:D], ALU.add
                                      ).then_inc(Q["acc_added"], 1)

            def moment(rows, mom):
                for i, row in enumerate(rows):
                    dve.bn_stats(stats[:, i, :], row)
                dve.drain()
                for i in range(len(rows)):
                    last = dve.bn_aggr(mom[:, i, :], stats[:, i, :])
                last.then_inc(S["var_ready"], 1)

            def invert(i, dev):
                dve.wait_ge(S["std_ready"], i + 1)
                dve.reciprocal(dev, dev)
                dve.drain()

            def spread(g):
                own = slice(g * UN, g * UN + UN)
                dve.wait_ge(s_x[g], 16 if g < NG - 1 else 32)
                moment([acc[:, t, :] for t in range(g * UN, g * UN + UN)], moments[:, own, :])

            def normalize(g):
                invert(g, rstd[:, g * UN:g * UN + UN, :])
                for u in range(UN):
                    t = g * UN + u
                    dve.wait_ge(S["tp_ready"], t + 1)
                    dve.tensor_scalar(xn[:, u, :], acc[:, t, :], moments[:, t, 0:1], rstd[:, t, :],
                                      ALU.subtract, ALU.mult).then_inc(S["xn_ready"], 1)

            def top(s):
                dve.tensor_reduce(rank_top[:, :], rank[:, bass.ds(s * CC, CC)], AX.X, ALU.max
                                  ).then_inc(S["top_ready"], 1)

            def keep_top(s):
                dve.wait_ge(S["top_t"], s + 1)
                dve.tensor_reduce(rank_new[:, :], b(7)[0:1, 0:EP], AX.X, ALU.max)
                dve.drain()
                dve.tensor_tensor(rank_run[:, :], rank_run[:, :], rank_new[:, :], ALU.max)
                dve.drain()
                dve.tensor_copy(rank_max[:, :], rank_run[:, :]).then_inc(S["max_ready"], 1)

            spread(0)
            dve.wait_ge(S["edges_in"], 48)
            for i, (data, op, by) in enumerate(((e_src, ALU.logical_shift_right, 7), (e_src, ALU.bitwise_and, 127),
                                                (e_dst, ALU.bitwise_and, HIGH), (e_dst, ALU.bitwise_and, LOW))):
                last = dve.tensor_scalar(e_bits[:, i, :], data[:, :], by, None, op)
            last.then_inc(S["bits_ready"], 1)
            normalize(0)
            spread(1)
            dve.wait_ge(S["const"], 1)
            dve.tensor_copy(iota_rank[:, :], iota_i[:, :])
            dve.tensor_scalar(valid[:, :], token1[:, :], float(N_NODES), None, ALU.is_le)
            dve.tensor_scalar(token_i[:, 1, :], token_i[:, 0, :], HIGH, None, ALU.bitwise_and)
            dve.tensor_scalar(token_i[:, 2, :], token_i[:, 0, :], LOW, None, ALU.bitwise_and)
            dve.drain()
            dve.tensor_copy(token_parts[:, :, :].rearrange("p n i -> p i n"), token_i[:, 1:3, :])
            normalize(1)
            spread(2)
            dve.wait_ge(S["parts_ready"], 1)
            block_hot(0)
            dve.sem_inc(S["block_ready"], 1)
            running_count(0)
            for g in range(2, NG):
                normalize(g)
                if g + 1 < NG:
                    spread(g + 1)
            place_count(0)
            top(0)
            for g in range(NG):
                build_piece(S, 0, g, g, rows=False)
            dve.wait_ge(S["more_in"], 16 * (KD + 5))
            dve.tensor_tensor(bias_sum[:, :], bias[:, 0, :], bias[:, 1, :], ALU.add).then_inc(S["bias_ready"], 1)
            take_table(S, 0, 0)
            keep_top(0)
            dve.wait_ge(S["h_stored"], NG * 16)
            weighted_hot(S, 0, 0)
            dve.wait_ge(S["wparts_ready"], 1)
            with dve.Fori(0, SC - 1) as s:
                n0 = s * NG
                block_hot(s + 1)
                running_count(s + 1)
                add_and_next(n0, 0, range(0, 2))
                place_count(s + 1)
                top(s + 1)
                add_and_next(n0, 0, range(2, UN))
                build_piece(S, s + 1, 0, n0 + NG)
                keep_top(s + 1)
                with dve.Fori(1, NG - 1) as g:
                    build_piece(S, s + 1, g, n0 + NG + g)
                    add_and_next(n0 + g, g)
                build_piece(S, s + 1, NG - 1, n0 + (2 * NG - 1))
                take_table(S, s + 1, s + 1)
                add_and_next(n0 + (NG - 1), NG - 1)
            dve.drain()
            dve.sem_inc(S["calm"], 1)

            def more(s, k):
                with dve.If(s == 0):
                    dve.tensor_scalar(rank[:, :], rank[:, :], float(-CAP), None, ALU.add)
                    dve.drain()
                block_hot(s)
                with dve.Fori(0, NG) as g:
                    build_piece(R, s, g, k * NG + g)
                take_table(R, SC, k)
                with dve.Fori(0, NG) as g:
                    weighted_hot(R, g + SC * NG, k * NG + g)
                    add_blocks(R, k * NG + g, g)
                for u in range(UN):
                    for j in range(NJ):
                        at = (SC - 1) * NG * UN * NJ + u * NJ + j
                        dve.tensor_scalar(hot[:, u * NJ + j, :], iota_node[:, :], t_src[:, at:at + 1],
                                          t_w[:, at:at + 1], ALU.is_equal, ALU.mult)
                dve.drain()
                dve.sem_inc(R["swept"], 1)

            more_rounds(dve, (("acc_added", UN),), more)
            dve.sem_inc(S["tail_ready"], 1)

            def smv(i):
                return sm[:, i, :, :]

            def wide(ap):
                return ap[:, :, None].broadcast_to([P, UN, N_EXP])

            rev5 = rev[:, None, :].broadcast_to([P, UN, N_EXP])
            MAXL, SUM, PRB, TOP, PLACE = (sc1[:, i, :] for i in range(5))

            def block(g, d, u, later):
                n = g + (SC - 1) * NG
                add_blocks(S, n, g, (u,))
                dve.drain()
                moment([acc[:, g * UN + u, :]], moments2[:, u:u + 1, :])
                if later:
                    weighted_hot(S, n + 1, n + 1, (u,))
                invert(g * UN + (NG + u), rstd2[:, u, :])
                dve.tensor_scalar(norm[:, d, u, :], acc[:, g * UN + u, :], moments2[:, u, 0:1],
                                  rstd2[:, u, :], ALU.subtract, ALU.mult).then_inc(S["x2_ready"], 1)

            def choose(g, d):
                dve.wait_ge(S["lg_ready"], g * UN + 2 * UN)
                dve.tensor_reduce(MAXL, LG[d], AX.X, ALU.max)
                dve.drain()
                dve.tensor_tensor(smv(0), LG[d], wide(MAXL), ALU.subtract).then_inc(S["lmax_ready"], 1)
                dve.wait_ge(S["exp_ready"], g + 1)
                dve.tensor_reduce(SUM, smv(1), AX.X, ALU.add)
                dve.drain()
                dve.reciprocal(SUM, SUM)
                dve.drain()
                dve.tensor_tensor(smv(2), smv(1), wide(SUM), ALU.mult)
                dve.drain()
                dve.tensor_reduce(PRB, smv(2), AX.X, ALU.max)
                dve.drain()
                dve.tensor_tensor(smv(3), smv(2), wide(PRB), ALU.is_equal)
                dve.drain()
                dve.tensor_tensor(smv(3), smv(3), rev5, ALU.mult)
                dve.drain()
                dve.tensor_reduce(TOP, smv(3), AX.X, ALU.max)
                dve.drain()
                dve.tensor_tensor(smv(4), rev5, wide(TOP), ALU.is_equal)
                dve.drain()
                dve.tensor_tensor(hot_e[:, :, :], smv(4), wide(valid[:, g * UN:(g + 1) * UN]), ALU.mult
                                  ).then_inc(S["hote_ready"], 1)

            def queue(g, d):
                dve.drain()
                dve.tensor_copy(entry[:, :, 0:2], token_parts[:, g * UN:(g + 1) * UN, :])
                dve.tensor_copy(entry[:, :, 2], PRB)
                dve.drain()
                dve.tensor_tensor(entry_rest[:, :], PRB, entry[:, :, 2], ALU.subtract)
                dve.drain()
                dve.tensor_copy(entry[:, :, 3], entry_rest[:, :])
                dve.drain()
                dve.tensor_tensor(entry[:, :, 4], entry_rest[:, :], entry[:, :, 3], ALU.subtract)
                dve.wait_ge(S["pos_ready"], g + 1)
                dve.tensor_tensor(smv(5), POS[d], hot_e[:, :, :], ALU.mult)
                dve.tensor_reduce(hot_new[:, :], hot_e[:, :, :].rearrange("p u e -> p e u"), AX.X, ALU.add)
                dve.drain()
                dve.tensor_tensor(hot_sum[:, :], hot_sum[:, :], hot_new[:, :], ALU.add)
                dve.tensor_reduce(PLACE, smv(5), AX.X, ALU.add)
                if g > 0:
                    dve.wait_ge(S["seat_done"], g)
                dve.tensor_tensor(entries[:, :, :].rearrange("p u (e i) -> p u e i", i=SEAT),
                                  hot_e[:, :, :, None].broadcast_to([P, UN, N_EXP, SEAT]),
                                  entry[:, :, None, :].broadcast_to([P, UN, N_EXP, SEAT]), ALU.mult)
                dve.drain()
                for u in range(UN):
                    last = dve.tensor_scalar(at_place[:, u, :], iota_rank[:, 0:ROWS_E], PLACE[:, u:u + 1], None,
                                             ALU.is_equal)
                last.then_inc(S["place_ready"], 1)

            for g in range(NG):
                if g > 1:
                    dve.wait_ge(s_rows[g % 2], 16 * (g // 2))
                for u in range(UN):
                    block(g, g % 2, u, g < NG - 1)
                    if u == 1 and g > 0:
                        choose(g - 1, (g - 1) % 2)
                    if u == 3 and g > 0:
                        queue(g - 1, (g - 1) % 2)
            choose(NG - 1, 0)
            queue(NG - 1, 0)

            def seat(i, n):
                return SEATS.rearrange("p (t e i) -> p e t i", e=N_EXP, i=SEAT)[:, :, :, i:i + n]

            dve.wait_ge(S["seats_ready"], 1)
            dve.tensor_reduce(seat_token[:, :, :], seat(0, 2), AX.X, ALU.add)
            dve.drain()
            dve.tensor_scalar(seat_from[:, :, :], seat_token[:, :, :], -1.0, 0.0, ALU.add, ALU.max
                              ).then_inc(S["from_ready"], 1)
            dve.tensor_scalar(seat_tmp[:, :, :], seat_token[:, :, :], 0.5, FAR, ALU.is_lt, ALU.mult)
            dve.tensor_reduce(seat_prob[:, :, :], seat(2, 3), AX.X, ALU.add)
            dve.drain()
            dve.scalar_tensor_tensor(out=seat_to[:, :, :], in0=seat_tmp[:, :, :], scalar=-1.0,
                                     in1=seat_token[:, :, :], op0=ALU.add, op1=ALU.add)
            dve.drain()
            dve.wait_ge(S["b2_in"], 16)

            for i in range(2):
                dve.wait_ge(s_rows[i], 16 * len(range(i, NG, 2)))
            dve.wait_ge(S["x1_out"], 16 * (NG + 1))
            for i in range(2):
                dve.tensor_copy(hid[:, i, :, EVEN:],
                                fills[:, 0, None, EVEN - ROWS_E:].broadcast_to([P, KF, ROWS_E - EVEN]))
            dve.drain()

            STEPS = 7

            def rows_rest(e):
                for k in range(KD):
                    dve.wait_ge(S["xn_hi"], 2 * e + (k + 1))
                    dve.tensor_tensor(xnT[:, 1, k, :], b(k), xnT[:, 0, k, :].bitcast(f32), ALU.subtract
                                      ).then_inc(S["xn_split"], 1)

            def tokens(e, s):
                dve.tensor_copy(row_to[:, s, :], seat_to[:, bass.ds(e, 1), :])
                dve.tensor_copy(prob[:, s, :], seat_prob[:, bass.ds(e, 1), :])
                dve.drain()

            def output(e, s, h, step, again=True):
                z = z_sb[:, 2 * h:2 * h + 2, :]
                if step == 0:
                    if again:
                        for t in (2 * h, 2 * h + 1):
                            dve.wait_ge(s_out[t], 16 * e)
                    dve.wait_ge(S["y_ready"], 2 * e + (h + 1))
                    dve.tensor_tensor(z, b(DOWN[h])[:, :].rearrange("p (t d) -> p t d", d=D),
                                      b2_all[:, bass.ds(e, 1), :].broadcast_to([P, 2, D]), ALU.add
                                      ).then_inc(S["y_read"], 1)
                elif step == 1:
                    for t in range(2 * h, 2 * h + 2):
                        dve.tensor_scalar(z_sb[:, t, :], z_sb[:, t, :], prob[:, s, t:t + 1], None, ALU.mult)
                elif step == 2:
                    dve.tensor_tensor(odd[:, 0, :, :], z, z, ALU.not_equal)
                elif step == 3:
                    dve.tensor_scalar(odd[:, 1, :, :], z, FLT_MAX, None, ALU.is_gt)
                    dve.tensor_scalar(odd[:, 2, :, :], z, -FLT_MAX, None, ALU.is_lt)
                else:
                    i = step - 4
                    last = dve.copy_predicated(z, odd[:, i, :, :], fills[:, i, None, :].broadcast_to([P, 2, D]))
                    if i == 2:
                        last.then_inc(S["z_ready"], 1)

            def hidden_rest(e, s, before=True, again=True):
                if before:
                    output(e - 1, 1 - s, 1, 0, again)
                for f in range(KF):
                    dve.wait_ge(S["relu_done"], 8 * e + (KF + f + 1))
                    dve.tensor_tensor(hid[:, 1, f, 0:EVEN], full[:, f % 2, 0:EVEN],
                                      hid[:, 0, f, 0:EVEN].bitcast(f32), ALU.subtract).then_inc(S["hid_split"], 1)
                    if before and f + 1 < STEPS:
                        dve.drain()
                        output(e - 1, 1 - s, 1, f + 1)

            def first_tiles(e, s, again=True):
                tokens(e, s)
                for step in range(STEPS):
                    output(e, s, 0, step, again)
                    dve.drain()

            def expert(e, s, again=True):
                rows_rest(e)
                first_tiles(e - 1, 1 - s, again)
                hidden_rest(e, s, again=again)

            rows_rest(0)
            hidden_rest(0, 0, before=False)
            expert(1, 1, again=False)
            expert(2, 0)
            with dve.Fori(1, (N_EXP - 2) // 2) as q:
                for s in range(2):
                    expert(2 * q + (1 + s), 1 - s)
            expert(N_EXP - 1, 1)
            first_tiles(N_EXP - 1, 1)
            for step in range(STEPS):
                output(N_EXP - 1, 1, 1, step)
                dve.drain()

    return nc


_INS = ['x', 'src', 'dst', 'edge_weight', 'L0_gnn_weight_l', 'L0_gnn_bias_l', 'L0_gnn_weight_r', 'L0_gnn_bias_r',
        'L0_ffn_gate_w', 'L0_ffn_gate_b', 'L0_ffn_w1', 'L0_ffn_b1', 'L0_ffn_w2', 'L0_ffn_b2']


def kernel(**inputs):
    import numpy as _np
    import concourse.bacc as _bacc
    from concourse import mybir as _mybir
    from concourse.bass_utils import run_bass_kernel_spmd as _run

    nc = _bacc.Bacc("TRN2", target_bir_lowering=False, num_devices=1)
    arrays, args = {}, []
    for name in _INS:
        a = _np.ascontiguousarray(inputs[name])
        arrays[f"in_{name}_dram"] = a
        args.append(nc.dram_tensor(f"in_{name}_dram", a.shape, _mybir.dt.from_np(a.dtype), kind="ExternalInput").ap())
    h_rows = nc.dram_tensor("h_rows", (NB * P, D), _mybir.dt.float32, kind="Internal").ap()
    norm_rows = nc.dram_tensor("norm_rows", (NB * P, D), _mybir.dt.float32, kind="Internal").ap()
    out = nc.dram_tensor("out_0_dram", (N_NODES, D), _mybir.dt.float32, kind="ExternalOutput").ap()
    graph_moe(nc, *args, h_rows, norm_rows, out)
    r = _run(nc, [arrays], core_ids=[0])
    return r.results[0]["out_0_dram"]
```
